# Optimizing a Trainium2 kernel written in Bass

```python
import numpy as np
import jax
import jax.numpy as jnp

def _softmax(x, axis=-1):
    return jax.nn.softmax(x, axis=axis)

def _gelu(x):
    return jax.nn.gelu(x, approximate=True)

def _silu(x):
    return jax.nn.silu(x)

def _sigmoid(x):
    return jax.nn.sigmoid(x)

def _layernorm(x, axis=-1, eps=1e-05):
    m = jnp.mean(x, axis=axis, keepdims=True)
    v = jnp.var(x, axis=axis, keepdims=True)
    return (x - m) / jnp.sqrt(v + eps)

def _scatter_add(tgt, idx, src, axis=0):
    return tgt.at[idx].add(src)

def _segment_sum(src, seg, n):
    return jax.ops.segment_sum(src, seg, n)
kernel_name = 'mk_decoder_preln_d1_seqx_r8_3c0315'

def setup_inputs(seed: int=0):
    np.random.seed(seed)
    _w = jnp.asarray

    def _rec_inputs():
        import jax
        import jax.numpy as jnp
        _rk = jax.random.key(seed)
        x = 7.22e-05 + 1 * jax.random.normal(jax.random.fold_in(_rk, 1), (8, 128, 512), jnp.float32)
        _lenS = 128 - jax.random.randint(jax.random.fold_in(_rk, 7), (8,), 0, max(1, 128 // 4) + 1, jnp.int32)
        _lenS2 = 128 - jax.random.randint(jax.random.fold_in(_rk, 8), (8,), 0, max(1, 128 // 4) + 1, jnp.int32)
        _ctx_4096P = jax.random.normal(jax.random.fold_in(_rk, 11), (8, 16, 512), jnp.float32)
        _ctx_4096c = jax.random.dirichlet(jax.random.fold_in(_rk, 511), 0.3 * jnp.ones((16,), jnp.float32), (8, 128))
        _ctx_4096t = jnp.einsum('bsk,bkd->bsd', _ctx_4096c, _ctx_4096P)
        _ctx_4096t = _ctx_4096t * jax.lax.rsqrt(jnp.mean(jnp.square(_ctx_4096t)) + 1e-12) * 0.953939
        ctx_4096 = 4.13588e-05 + 0.999923 * (_ctx_4096t + 0.3 * jax.random.normal(jax.random.fold_in(_rk, 611), (8, 128, 512), jnp.float32))
        return (x, ctx_4096)
    x, ctx_4096 = _rec_inputs()

    def _L0_attn_setup():
        import jax, jax.numpy as jnp
        import numpy as np
        H = 512
        D_IN = 1024
        N = 16
        K = 4
        R = 32
        EPS = 1e-06

        def rms_forward(x, eps=EPS):
            xf = x.astype(jnp.float32)
            var = jnp.mean(xf * xf, axis=-1, keepdims=True)
            return (xf * jax.lax.rsqrt(var + eps)).astype(x.dtype)
        key = jax.random.key(seed)
        ks = jax.random.split(key, 10)
        s = 0.02
        hidden_states = jax.random.normal(ks[0], (2, 128, H), dtype=jnp.float32)
        W_in = jax.random.normal(ks[1], (2 * D_IN, H), dtype=jnp.float32) * s
        conv_w = jax.random.normal(ks[2], (D_IN, K), dtype=jnp.float32) * 0.2
        conv_b = jax.random.normal(ks[3], (D_IN,), dtype=jnp.float32) * 0.02
        W_x = jax.random.normal(ks[4], (R + 2 * N, D_IN), dtype=jnp.float32) * s
        W_dt = jax.random.normal(ks[5], (D_IN, R), dtype=jnp.float32) * s
        b_dt = jax.random.normal(ks[6], (D_IN,), dtype=jnp.float32) * 0.02
        A_log = jnp.log(jnp.broadcast_to(jnp.arange(1, N + 1, dtype=jnp.float32)[None, :], (D_IN, N)))
        D = jnp.ones((D_IN,), dtype=jnp.float32)
        W_out = jax.random.normal(ks[7], (H, D_IN), dtype=jnp.float32) * s
        return {'hidden_states': hidden_states, 'W_in': W_in, 'conv_w': conv_w, 'conv_b': conv_b, 'W_x': W_x, 'W_dt': W_dt, 'b_dt': b_dt, 'A_log': A_log, 'D': D, 'W_out': W_out}
    _L0_attn_all = _L0_attn_setup()
    _L0_attn_in = {k: v for k, v in _L0_attn_all.items() if k in ('W_in', 'conv_w', 'conv_b', 'W_x', 'W_dt', 'b_dt', 'A_log', 'D', 'W_out')}
    del _L0_attn_all

    def _L0_xattn_setup():
        import jax, jax.numpy as jnp
        import numpy as np
        B, S, D = (1, 256, 512)
        H, HKV, DK, DV = (32, 8, 128, 128)
        key = jax.random.key(seed)
        ks = jax.random.split(key, 7)
        std = 0.02
        return {'q': jax.random.normal(ks[0], (B, S, D), jnp.float32), 'k': jax.random.normal(ks[1], (B, S, D), jnp.float32), 'v': jax.random.normal(ks[2], (B, S, D), jnp.float32), 'Wq': jax.random.normal(ks[3], (H * DK, D), jnp.float32) * std, 'Wk': jax.random.normal(ks[4], (HKV * DK, D), jnp.float32) * std, 'Wv': jax.random.normal(ks[5], (HKV * DV, D), jnp.float32) * std, 'Wd': jax.random.normal(ks[6], (D, H * DV), jnp.float32) * std}
    _L0_xattn_all = _L0_xattn_setup()
    _L0_xattn_in = {k: v for k, v in _L0_xattn_all.items() if k in ('Wq', 'Wk', 'Wv', 'Wd')}
    del _L0_xattn_all

    def _L0_ffn_setup():
        import jax, jax.numpy as jnp
        import numpy as np
        IN_F = 512
        OUT_F = 512
        RANK = 8
        NUM_EXPERTS = 64
        TOP_K = 16
        ROUTER_DIM = 16
        ALPHA = 32
        SCALING = ALPHA / TOP_K
        BOTTLENECK = NUM_EXPERTS * RANK
        key = jax.random.key(seed)
        ks = jax.random.split(key, 5)
        x = jax.random.normal(ks[0], (4, 512, IN_F), dtype=jnp.float32)
        bound_a = float(np.sqrt(6.0 / IN_F))
        A_w = jax.random.uniform(ks[1], (BOTTLENECK, IN_F), jnp.float32, -bound_a, bound_a)
        B_w = jax.random.normal(ks[2], (OUT_F, BOTTLENECK), dtype=jnp.float32) * 0.02
        Wq_w = jax.random.normal(ks[3], (ROUTER_DIM, IN_F), dtype=jnp.float32) * 0.02
        keys = jax.random.normal(ks[4], (NUM_EXPERTS, ROUTER_DIM), dtype=jnp.float32) * 0.01
        return {'x': x, 'A_w': A_w, 'B_w': B_w, 'Wq_w': Wq_w, 'keys': keys}
    _L0_ffn_all = _L0_ffn_setup()
    _L0_ffn_in = {k: v for k, v in _L0_ffn_all.items() if k in ('A_w', 'B_w', 'Wq_w', 'keys')}
    del _L0_ffn_all
    return {'x': x, 'ctx_4096': ctx_4096, 'L0_attn_W_in': _L0_attn_in['W_in'], 'L0_attn_conv_w': _L0_attn_in['conv_w'], 'L0_attn_conv_b': _L0_attn_in['conv_b'], 'L0_attn_W_x': _L0_attn_in['W_x'], 'L0_attn_W_dt': _L0_attn_in['W_dt'], 'L0_attn_b_dt': _L0_attn_in['b_dt'], 'L0_attn_A_log': _L0_attn_in['A_log'], 'L0_attn_D': _L0_attn_in['D'], 'L0_attn_W_out': _L0_attn_in['W_out'], 'L0_xattn_Wq': _L0_xattn_in['Wq'], 'L0_xattn_Wk': _L0_xattn_in['Wk'], 'L0_xattn_Wv': _L0_xattn_in['Wv'], 'L0_xattn_Wd': _L0_xattn_in['Wd'], 'L0_ffn_A_w': _L0_ffn_in['A_w'], 'L0_ffn_B_w': _L0_ffn_in['B_w'], 'L0_ffn_Wq_w': _L0_ffn_in['Wq_w'], 'L0_ffn_keys': _L0_ffn_in['keys']}

def reference(x, ctx_4096, L0_attn_W_in, L0_attn_conv_w, L0_attn_conv_b, L0_attn_W_x, L0_attn_W_dt, L0_attn_b_dt, L0_attn_A_log, L0_attn_D, L0_attn_W_out, L0_xattn_Wq, L0_xattn_Wk, L0_xattn_Wv, L0_xattn_Wd, L0_ffn_A_w, L0_ffn_B_w, L0_ffn_Wq_w, L0_ffn_keys):
    import jax
    import jax.numpy as jnp

    def _L0_attn_ref(hidden_states, W_in, conv_w, conv_b, W_x, W_dt, b_dt, A_log, D, W_out):
        import jax, jax.numpy as jnp
        import numpy as np
        H = 512
        D_IN = 1024
        N = 16
        K = 4
        R = 32
        EPS = 1e-06

        def rms_forward(x, eps=EPS):
            xf = x.astype(jnp.float32)
            var = jnp.mean(xf * xf, axis=-1, keepdims=True)
            return (xf * jax.lax.rsqrt(var + eps)).astype(x.dtype)
        b, L, _ = hidden_states.shape
        proj = hidden_states @ W_in.T
        x, gate = (proj[..., :D_IN], proj[..., D_IN:])
        xpad = jnp.pad(x, ((0, 0), (K - 1, 0), (0, 0)))
        xc = conv_b
        for j in range(K):
            xc = xc + conv_w[:, j] * xpad[:, j:j + L, :]
        x = jax.nn.silu(xc)
        ssm = x @ W_x.T
        ts, Bm, Cm = (ssm[..., :R], ssm[..., R:R + N], ssm[..., R + N:])
        ts = rms_forward(ts)
        Bm = rms_forward(Bm)
        Cm = rms_forward(Cm)
        dt = jax.nn.softplus(ts @ W_dt.T + b_dt)
        A = -jnp.exp(A_log.astype(jnp.float32))

        def step(state, inp):
            dt_t, B_t, C_t, u_t = inp
            dA = jnp.exp(dt_t[..., None] * A)
            state = state * dA + (dt_t * u_t)[..., None] * B_t[:, None, :]
            y = jnp.einsum('bdn,bn->bd', state, C_t)
            return (state, y)
        init = jnp.zeros((b, D_IN, N), dtype=jnp.float32)
        xs = (dt.transpose(1, 0, 2), Bm.transpose(1, 0, 2), Cm.transpose(1, 0, 2), x.transpose(1, 0, 2))
        _, ys = jax.lax.scan(step, init, xs)
        y = ys.transpose(1, 0, 2) + x * D
        y = y * jax.nn.silu(gate)
        return y @ W_out.T

    def _L0_xattn_ref(q, k, v, Wq, Wk, Wv, Wd):
        import jax, jax.numpy as jnp
        import numpy as np
        B, S, D = (1, 256, 512)
        H, HKV, DK, DV = (32, 8, 128, 128)
        b, s, _ = q.shape
        exp = H // HKV
        Q = (q @ Wq.T).reshape(b, s, HKV, exp, DK)
        K = (k @ Wk.T).reshape(b, s, HKV, DK)
        V = (v @ Wv.T).reshape(b, s, HKV, DV)
        scale = DK ** (-0.5)
        scores = jnp.einsum('bqhed,bkhd->bheqk', Q, K) * scale
        causal = jnp.tril(jnp.ones((s, s), dtype=bool))
        scores = jnp.where(causal, scores, jnp.finfo(scores.dtype).min)
        probs = jax.nn.softmax(scores, axis=-1)
        attn = jnp.einsum('bheqk,bkhd->bqhed', probs, V)
        attn = attn.reshape(b, s, H * DV)
        return attn @ Wd.T

    def _L0_ffn_ref(x, A_w, B_w, Wq_w, keys):
        import jax, jax.numpy as jnp
        import numpy as np
        IN_F = 512
        OUT_F = 512
        RANK = 8
        NUM_EXPERTS = 64
        TOP_K = 16
        ROUTER_DIM = 16
        ALPHA = 32
        SCALING = ALPHA / TOP_K
        BOTTLENECK = NUM_EXPERTS * RANK
        q = jnp.einsum('bsd,rd->bsr', x, Wq_w)
        scores = jnp.einsum('bsr,er->bse', q, keys)
        top_vals, top_idx = jax.lax.top_k(scores, TOP_K)
        top_w = jax.nn.softmax(top_vals, axis=-1)
        gate = jnp.sum(jax.nn.one_hot(top_idx, NUM_EXPERTS, dtype=top_w.dtype) * top_w[..., None], axis=-2)
        z = jnp.einsum('bsd,nd->bsn', x, A_w)
        z = z.reshape(*z.shape[:-1], NUM_EXPERTS, RANK)
        z_gated = (z * gate[..., None]).reshape(*z.shape[:-2], BOTTLENECK)
        out = jnp.einsum('bsn,on->bso', z_gated, B_w) * SCALING
        return out
    x = x + _L0_attn_ref(_layernorm(x, axis=-1), L0_attn_W_in, L0_attn_conv_w, L0_attn_conv_b, L0_attn_W_x, L0_attn_W_dt, L0_attn_b_dt, L0_attn_A_log, L0_attn_D, L0_attn_W_out)
    x = x + _L0_xattn_ref(_layernorm(x, axis=-1), ctx_4096, ctx_4096, L0_xattn_Wq, L0_xattn_Wk, L0_xattn_Wv, L0_xattn_Wd)
    x = x + _L0_ffn_ref(_layernorm(x, axis=-1), L0_ffn_A_w, L0_ffn_B_w, L0_ffn_Wq_w, L0_ffn_keys)
    return x

_drawn_inputs = setup_inputs


def setup_inputs(seed=0):
    import zlib

    import numpy as np

    out = dict(_drawn_inputs(seed))
    spreads = {'L0_attn_D': (1.0, 0.6)}
    factors = {'L0_attn_conv_b': 7.477,
     'L0_attn_W_dt': 8.0,
     'L0_attn_b_dt': 59.034,
     'L0_attn_A_log': 32.406}
    for name, (base, spread) in spreads.items():
        noise = np.random.default_rng([zlib.crc32(name.encode()), seed]).standard_normal(out[name].shape)
        drawn = base * np.exp(spread * noise) if base else spread * noise
        out[name] = jnp.asarray(drawn.astype(out[name].dtype))
    for name, factor in factors.items():
        out[name] = (out[name] * factor).astype(out[name].dtype)
    return out
```

```python
from contextlib import ExitStack

import numpy as np

import concourse.bass as bass
from concourse import mybir

F32 = mybir.dt.float32
F32R = mybir.dt.float32r
ALU = mybir.AluOpType
ACT = mybir.ActivationFunctionType
AX_X = mybir.AxisListType.X

P = 128
BATCH, SEQ, DM = 8, 128, 512
TOK = BATCH * SEQ
HALF = TOK // 2
NB = HALF // P
KT = DM // P
DIN = 1024
NC = DIN // P
NS = 16
RDT = 32
SSM = RDT + 2 * NS
TAPS = 4
G, HPG, DK = 8, 4, 128
EXPERTS, RANK, TOPK, RDIM = 64, 8, 16, 16
CH_N = 2
CHUNKS = NS // CH_N
CST = NS + TAPS + 3
CONV0, CONVB, DTB, DSKIP = NS, NS + TAPS, NS + TAPS + 1, NS + TAPS + 2
LN_EPS, RMS_EPS = 1e-5, 1e-6
MASKED = -1e30
NEG = -3.0e38
A_LOG_MAX = 80.0

HL_LN1 = 0
HL_SSM = HL_LN1 + 2 * KT
HL_KV = HL_SSM + 2
HL_LN2 = [HL_KV + 4 * G, 0]
XSTEP = 2 * NB + HPG
HL_Q = [HL_LN2[0] + KT, 0]
HL_X = [HL_Q[0] + HPG, 0]
HL_LN2[1] = HL_X[0] + XSTEP * G - HPG
HL_Q[1] = HL_LN2[1] + KT
HL_X[1] = HL_Q[1] + HPG
HL_LN3 = [HL_X[1] + XSTEP * G - HPG + 2 * KT * h for h in range(2)]
HL_ZT = [n + KT for n in HL_LN3]

S_IN = 0
S_BC = [S_IN + 4 * NC, S_IN + 4 * NC + NS]
S_X = [S_BC[1] + NS, S_BC[1] + NS + NB * G]
S_FFN = S_X[1] + NB * G

D_IN = 0
D_BC = [D_IN + 2 * NC, 0]
D_SCAN = [D_BC[0] + NS, 0]
D_BC[1] = D_SCAN[0] + NB * NC
D_SCAN[1] = D_BC[1] + NS
D_X = [D_SCAN[1] + NB * NC, 0]
D_X[1] = D_X[0] + NB * G
D_FFN = D_X[1] + NB * G

R_WX = 0
R_IN = R_WX + 1
R_CTX = R_IN + 2 * NC
R_KV = R_CTX + 2 * KT
R_Q = [R_KV + 2 * G, 0]
R_X = [R_Q[0] + HPG, 0]
R_Q[1] = R_X[0] + 2 * HPG * G - HPG
R_X[1] = R_Q[1] + HPG
R_FFN = R_X[1] + 2 * HPG * G - HPG
R_FFN_N = 1 + 2 * KT


def use(base, per, i, k):
    n = base + k
    return n % 2, n // 2 + (per // 2) * i


class Chain:

    def __init__(self, eng, sem, per, step):
        self.eng, self.sem, self.per, self.step, self.n = eng, sem, per, step, 0

    def did(self, ins):
        ins.then_inc(self.sem, 1)
        self.n += 1

    def wait(self):
        self.eng.wait_ge(self.sem, self.per * self.step + self.n)

    def end(self):
        assert self.n == self.per, (self.n, self.per)


def steps(eng, body):
    with eng.Fori(0, NC // 2 - 1) as i:
        body(i, 0, True)
        body(i, 1, True)
    body(NC // 2 - 1, 0, True)
    body(NC // 2 - 1, 1, False)


def bass_decoder(nc, x, w_in, cst, w_x, w_dt, w_out, ctx_t, w_kv, w_q, w_d, w_a, w_b, w_r, keys, out):
    ctx = ExitStack()
    with ctx:
        def sb(name, shape, dt=F32, scope=ctx):
            return scope.enter_context(nc.sbuf_tensor(name, shape, dt))

        def sem(name):
            return ctx.enter_context(nc.semaphore(name))

        def sem2(name, n=2):
            return [sem(f"{name}{k}") for k in range(n)]

        banks = [ctx.enter_context(nc.psum_tensor(f"bank{k}", [P, HALF], F32)) for k in range(8)]
        hl_bank, s_bank, d_bank, dt_bank, y_bank = banks[0:2], banks[2:4], banks[4:6], banks[6], banks[7]

        xres = sb("xres", [P, 2 * NB, DM])
        xt_hi = sb("xt_hi", [P, KT, HALF], F32R)
        xt_lo = sb("xt_lo", [P, KT, HALF], F32R)
        ident = sb("ident", [P, P])
        ident_r = sb("ident_r", [P, P], F32R)
        mask = sb("mask", [P, P])
        mask_r = sb("mask_r", [P, P], F32R)
        raw = sb("raw", [P, 2, DM])
        ring_hi = sb("ring_hi", [P, 2, DM], F32R)
        ring_lo = sb("ring_lo", [P, 2, DM], F32R)
        cst_sb = sb("cst_sb", [P, 2, CST])
        stats = sb("stats", [P, NB, 6])
        mv = sb("mv", [P, NB, 2])
        lnv = sb("lnv", [P, NB])
        rstd = sb("rstd", [P, NB])
        eps_ln = sb("eps_ln", [P, 1])
        eps_rms = sb("eps_rms", [P, 1])
        da = sb("da", [P, 2, CH_N, HALF])
        ch = sb("ch", [P, 4, CH_N * HALF])
        xn = ch[:, 0:2, :].rearrange("p a (b d) -> p (a b) d", d=DM)
        stk = sb("stk", [P, 2, HALF], F32R)

        u_dram = nc.dram_tensor("u_spill", [2, NC, P, HALF], F32, kind="Internal").ap()
        sg_dram = nc.dram_tensor("sg_spill", [2, NC, P, HALF], F32, kind="Internal").ap()
        kv_dram = nc.dram_tensor("kv_spill", [G, 4, 2, P, HALF], F32, kind="Internal").ap()

        def scan_buffers(scope):
            return dict(
                bc=sb("bc", [P, 2 * NS, HALF], F32, scope),
                u=sb("u_in", [P, 2, HALF], F32, scope),
                sg=sb("sg_in", [P, HALF], F32, scope),
                wdt=sb("wdt", [P, P], F32, scope),
                wdt_hi=sb("wdt_hi", [P, P], F32R, scope),
                wdt_lo=sb("wdt_lo", [P, P], F32R, scope),
                wo=sb("wo", [P, DM], F32, scope),
                wo_hi=sb("wo_hi", [P, DM], F32R, scope),
                wo_lo=sb("wo_lo", [P, DM], F32R, scope),
                ea=sb("ea", [P, 2, NS], F32, scope),
                na=sb("na", [P, 2, NS], F32, scope),
                dt=sb("dt", [P, HALF], F32, scope),
                dtu=sb("dtu", [P, HALF], F32, scope),
                sp=sb("sp", [P, HALF], F32, scope),
                rl=sb("rl", [P, HALF], F32, scope),
                y=sb("y", [P, HALF], F32, scope),
                y_hi=sb("y_hi", [P, HALF], F32R, scope),
                y_lo=sb("y_lo", [P, HALF], F32R, scope),
            )

        with ExitStack() as sc:
            xt1_hi = sb("xt1_hi", [P, KT, HALF], F32R, sc)
            xt1_lo = sb("xt1_lo", [P, KT, HALF], F32R, sc)
            wx_hi = sb("wx_hi", [P, NC * SSM], F32R, sc)
            wx_lo = sb("wx_lo", [P, NC * SSM], F32R, sc)
            xpad = sb("xpad", [P, 2, NB, TAPS - 1 + SEQ], F32, sc)
            conv = sb("conv", [P, 2, HALF], F32, sc)
            u_out = sb("u_out", [P, 2, 2, HALF], F32, sc)
            sg_out = sb("sg_out", [P, 2, 2, HALF], F32, sc)
            u_hi = sb("u_hi", [P, 2, HALF], F32R, sc)
            u_lo = sb("u_lo", [P, 2, HALF], F32R, sc)
            ssm = sb("ssm", [P, 2 * NB, SSM], F32, sc)
            ssm_sq = sb("ssm_sq", [P, 2 * NB, SSM], F32, sc)
            ssm_n = sb("ssm_n", [P, 2 * NB, 2, SSM], F32, sc)
            ssm_ss = sb("ssm_ss", [P, 3, 2 * NB], F32, sc)
            ssm_ln = sb("ssm_ln", [P, 3, 2 * NB], F32, sc)
            ssm_rs = sb("ssm_rs", [P, 3, 2 * NB], F32, sc)
            stk_t = sb("stk_t", [P, HALF], F32R, sc)

        sc_scan = ExitStack()
        B = scan_buffers(sc_scan)
        with ExitStack() as sc:
            ctx_hi = sb("ctx_hi", [P, KT, TOK], F32R, sc)
            ctx_lo = sb("ctx_lo", [P, KT, TOK], F32R, sc)
            stg_hi = sb("stg_hi", [P, 2, HALF], F32R, sc)
            stg_lo = sb("stg_lo", [P, 2, HALF], F32R, sc)
            sel_c = sb("sel_c", [P, 2 * NS], F32, sc)
            sel = sb("sel", [P, 2 * NS, P], F32R, sc)
        with ExitStack() as sc:
            q_hi = sb("q_hi", [P, HPG, HALF], F32R, sc)
            q_lo = sb("q_lo", [P, HPG, HALF], F32R, sc)
            kv = sb("kv", [P, 2, 2, HALF], F32R, sc)
            pr = sb("pr", [P, 2, HPG, P], F32, sc)
            pt_hi = sb("pt_hi", [P, HALF], F32R, sc)
            pt_lo = sb("pt_lo", [P, HALF], F32R, sc)
            at_hi = sb("at_hi", [P, 2, HALF], F32R, sc)
            at_lo = sb("at_lo", [P, 2, HALF], F32R, sc)
            wd_hi = sb("wd_hi", [P, HPG, DM], F32R, sc)
            wd_lo = sb("wd_lo", [P, HPG, DM], F32R, sc)
            mx = sb("mx", [P, 2, HPG], F32, sc)
            nmx = sb("nmx", [P, 2, HPG], F32, sc)
            psum_row = sb("psum_row", [P, 2, HPG], F32, sc)
            rcp = sb("rcp", [P, 2, HPG], F32, sc)
        sc_scan.close()
        with ExitStack() as sc:
            a_hi = sb("a_hi", [P, KT, DM], F32R, sc)
            a_lo = sb("a_lo", [P, KT, DM], F32R, sc)
            b_hi = sb("b_hi", [P, KT, DM], F32R, sc)
            b_lo = sb("b_lo", [P, KT, DM], F32R, sc)
            r_hi = sb("r_hi", [P, DM], F32R, sc)
            r_lo = sb("r_lo", [P, DM], F32R, sc)
            keys_sb = sb("keys_sb", [P, EXPERTS], F32, sc)
            qr = sb("qr", [P, HALF], F32, sc)
            sco = sb("sco", [P, NB, EXPERTS], F32, sc)
            sco1 = sb("sco1", [P, NB, EXPERTS], F32, sc)
            sco2 = sb("sco2", [P, NB, EXPERTS], F32, sc)
            top = sb("top", [P, NB, 2, 8], F32, sc)
            ntop = sb("ntop", [P, NB], F32, sc)
            gsum = sb("gsum", [P, NB], F32, sc)
            grcp = sb("grcp", [P, NB], F32, sc)
            picked = sb("picked", [P, NB, EXPERTS], F32, sc)
            ge = sb("ge", [P, NB, EXPERTS], F32, sc)
            zg = sb("zg", [P, NB, DM], F32, sc)
            zt_hi = sb("zt_hi", [P, KT, HALF], F32R, sc)
            zt_lo = sb("zt_lo", [P, KT, HALF], F32R, sc)
            res = sb("res", [P, 2 * NB, DM], F32, sc)

        x_in, const_ok, masks_ok = sem2("x_in"), sem("const_ok"), sem("masks_ok")
        hl_full, hl_hi, hl_free = sem2("hl_full"), sem2("hl_hi"), sem2("hl_free")
        s_full, s_free = sem2("s_full"), sem2("s_free")
        d_full, d_free = sem2("d_full"), sem2("d_free")
        raw_in, w_hi_ok, w_ok = sem2("raw_in"), sem2("w_hi_ok"), sem2("w_ok")
        ln_mv, ln_stat, ln_rstd, ln_xn = sem("ln_mv"), sem("ln_stat"), sem("ln_rstd"), sem("ln_xn")
        cst_in = sem2("cst_in")
        pad_ok, conv_ch, conv_ok, silu_ok = sem("pad_ok"), sem("conv_ch"), sem("conv_ok"), sem("silu_ok")
        uhi_ok, ulo_ok, gate_ok = sem("uhi_ok"), sem("ulo_ok"), sem("gate_ok")
        spill = sem2("spill")
        ssm_ch, ssm_rs_ok, stk_cp = sem("ssm_ch"), sem("ssm_rs_ok"), sem("stk_cp")
        stg_out = sem2("stg_out")
        sel_ok, zero_ok = sem("sel_ok"), sem("zero_ok")
        scan_in, sg_in, ws_in = sem2("scan_in"), sem("sg_in"), sem("ws_in")
        wdt_hi_ok, wdt_ok, wo_hi_ok, wo_ok = sem("wdt_hi_ok"), sem("wdt_ok"), sem("wo_hi_ok"), sem("wo_ok")
        dt_full, dt_abs, dt_free, dt_exp, dt_ln = (sem("dt_full"), sem("dt_abs"), sem("dt_free"), sem("dt_exp"),
                                                   sem("dt_ln"))
        al_ok, dt_err, dt_rest = sem("al_ok"), sem("dt_err"), sem("dt_rest")
        ea_ok, na_ok, dt_ok, dtu_ok = sem("ea_ok"), sem("na_ok"), sem("dt_ok"), sem("dtu_ok")
        da_full, scan_done = sem2("da_full"), sem2("scan_done")
        ch_full, ch_mul, ch_free = sem2("ch_full", 4), sem2("ch_mul", 4), sem2("ch_free", 4)
        y_full, y_free, y_ok, yhi_ok, ylo_ok = (sem("y_full"), sem("y_free"), sem("y_ok"), sem("yhi_ok"),
                                                sem("ylo_ok"))
        kv_in, mx_ch, mx_ok, sum_ok, rcp_ok, pn_ok = (sem("kv_in"), sem("mx_ch"), sem("mx_ok"), sem("sum_ok"),
                                                      sem("rcp_ok"), sem("pn_ok"))
        keys_in, qr_ok, ffn_ch, ge_ok, gate_f, zg_ok, out_ok, stored = (
            sem("keys_in"), sem("qr_ok"), sem("ffn_ch"), sem("ge_ok"), sem("gate_f"), sem("zg_ok"),
            sem("out_ok"), sem("stored"))
        block = ctx.enter_context(nc.Block())

        @block.sync
        def _(eng):
            def ring_load(base, per, i, k, src):
                slot, n = use(base, per, i, k)
                eng.wait_ge(w_ok[slot], n)
                eng.dma_start(raw[:, slot, :], src).then_inc(raw_in[slot], 16)

            eng.dma_start(xres[:, 0:NB, :], x[0]).then_inc(x_in[0], 16)
            ring_load(R_WX, 0, 0, 0, w_x)
            ring_load(R_IN, 2, 0, 0, w_in[0, 0])
            eng.dma_start(xres[:, NB:2 * NB, :], x[1]).then_inc(x_in[1], 16)
            eng.dma_start(cst_sb[:, 0, :], cst[0]).then_inc(cst_in[0], 16)
            ring_load(R_IN, 2, 0, 1, w_in[0, 1])

            def in_step(i, p, nxt):
                c = 2 * i + p
                if nxt:
                    if p == 0:
                        eng.wait_ge(conv_ok, 4 * i)
                    else:
                        eng.wait_ge(conv_ok, 4 * i + 2)
                    eng.dma_start(cst_sb[:, 1 - p, :], cst[c + 1]).then_inc(cst_in[1 - p], 16)
                    for k in range(2):
                        ring_load(R_IN + 2 * p, 4, i, 2 + k, w_in[c + 1, k])
                eng.wait_ge(gate_ok, 2 * c + 2)
                for h in range(2):
                    eng.dma_start(sg_dram[h, c], sg_out[:, p, h, :]).then_inc(spill[p], 16)
                eng.wait_ge(silu_ok, 2 * c + 2)
                for h in range(2):
                    eng.dma_start(u_dram[h, c], u_out[:, p, h, :]).then_inc(spill[p], 16)
            steps(eng, in_step)

            for k in range(2 * KT):
                ring_load(R_CTX, 0, 0, k, ctx_t[k])
            for k in range(2):
                ring_load(R_KV, 2, 0, k, w_kv[0, k])

            for p in range(2):
                eng.wait_ge(spill[p], 4 * 16 * (NC // 2))
            eng.wait_ge(hl_free[0], HL_KV // 2)
            eng.wait_ge(hl_free[1], HL_KV // 2)

            def kv_step(i, p, nxt):
                g = 2 * i + p
                if nxt:
                    for k in range(2):
                        ring_load(R_KV + 2 * p, 4, i, 2 + k, w_kv[g + 1, k])
                for k in range(4):
                    slot, n = use(HL_KV + 4 * p, 8, i, k)
                    eng.wait_ge(hl_free[slot], n + 1)
                    eng.dma_start(kv_dram[g, k, 0], stg_hi[:, slot, :].bitcast(F32)).then_inc(stg_out[slot], 16)
                    eng.dma_start(kv_dram[g, k, 1], stg_lo[:, slot, :].bitcast(F32)).then_inc(stg_out[slot], 16)

            def scan_load(h, i, p):
                c, s = 2 * i + p, NC * h + 2 * i + p
                if h or not isinstance(i, int) or s >= 2:
                    eng.wait_ge(y_free, s - 1)
                eng.dma_start(B["u"][:, p, :], u_dram[h, c]).then_inc(scan_in[p], 16)
                eng.dma_start(cst_sb[:, p, :], cst[c]).then_inc(scan_in[p], 16)
                eng.wait_ge(wdt_ok, s)
                eng.dma_start(B["wdt"][:, :], w_dt[c]).then_inc(ws_in, 16)

            def scan_step(h, i, p, nxt):
                c, s = 2 * i + p, NC * h + 2 * i + p
                eng.wait_ge(wo_ok, s)
                eng.wait_ge(y_ok, s)
                eng.dma_start(B["sg"][:, :], sg_dram[h, c]).then_inc(sg_in, 16)
                eng.dma_start(B["wo"][:, :], w_out[c]).then_inc(sg_in, 16)
                if nxt:
                    if p == 0:
                        scan_load(h, i, 1)
                    else:
                        scan_load(h, i + 1, 0)

            steps(eng, kv_step)
            scan_load(0, 0, 0)
            steps(eng, lambda i, p, nxt: scan_step(0, i, p, nxt))
            scan_load(1, 0, 0)
            steps(eng, lambda i, p, nxt: scan_step(1, i, p, nxt))

            for p in range(2):
                eng.wait_ge(stg_out[p], 2 * 16 * (4 * G // 2))

            def x_step(h, i, p, nxt):
                g, s = 2 * i + p, G * h + 2 * i + p
                slot, n = use(HL_X[h] + XSTEP * p, 2 * XSTEP, i, 0)
                if h or not isinstance(i, int) or p or i:
                    eng.wait_ge(hl_full[1], use(HL_X[h] + XSTEP * p, 2 * XSTEP, i, -XSTEP + 9)[1] + 1)
                for k in range(2):
                    for l in range(2):
                        eng.dma_start(kv[:, k, l, :].bitcast(F32), kv_dram[g, 2 * k + h, l]).then_inc(kv_in, 16)
                for j in range(HPG):
                    ring_load(R_X[h] + 2 * HPG * p, 4 * HPG, i, j, w_d[g, j])
                if nxt:
                    for j in range(HPG):
                        ring_load(R_X[h] + 2 * HPG * p, 4 * HPG, i, HPG + j, w_q[g + 1, j])

            for h in range(2):
                for j in range(HPG):
                    ring_load(R_Q[h], 0, 0, j, w_q[0, j])
                steps(eng, lambda i, p, nxt: x_step(h, i, p, nxt))

            ring_load(R_FFN, 0, 0, 0, w_r)
            for k in range(KT):
                ring_load(R_FFN, 0, 0, 1 + k, w_a[k])
            for k in range(KT):
                ring_load(R_FFN, 0, 0, 1 + KT + k, w_b[k])
            for p in range(2):
                eng.wait_ge(hl_full[p], HL_LN3[0] // 2)
            eng.dma_start(keys_sb[:, :], keys).then_inc(keys_in, 16)
            for h in range(2):
                eng.wait_ge(out_ok, NB * (h + 1))
                eng.dma_start(out[h], res[:, NB * h:NB * (h + 1), :]).then_inc(stored, 16)
            eng.wait_ge(stored, 32)

        @block.gpsimd
        def _(eng):
            eng.memset(ident[:, :], 0.0).then_inc(const_ok, 1)
            eng.memset(mask[:, :], 0.0).then_inc(const_ok, 1)
            eng.memset(eps_ln[:, :], LN_EPS).then_inc(const_ok, 1)
            eng.memset(eps_rms[:, :], RMS_EPS).then_inc(const_ok, 1)
            eng.wait_ge(const_ok, 4)
            eng.affine_select(out=ident[:, :], in_=ident[:, :], compare_op=ALU.not_equal, fill=1.0, base=0,
                              pattern=[[-1, P]], channel_multiplier=1).then_inc(const_ok, 1)
            eng.affine_select(out=mask[:, :], in_=mask[:, :], compare_op=ALU.is_ge, fill=MASKED, base=0,
                              pattern=[[-1, P]], channel_multiplier=1).then_inc(const_ok, 1)

            def ring_lo_part(base, per, i, k, lo, hi):
                slot, n = use(base, per, i, k)
                eng.wait_ge(w_hi_ok[slot], n + 1)
                nc.gpsimd.tensor_tensor(lo, raw[:, slot, :], hi, ALU.subtract).then_inc(w_ok[slot], 1)

            ring_lo_part(R_WX, 0, 0, 0, wx_lo[:, :], wx_hi[:, :].bitcast(F32))
            for k in range(2):
                ring_lo_part(R_IN, 2, 0, k, ring_lo[:, k, :], ring_hi[:, k, :].bitcast(F32))

            def in_step(i, p, nxt):
                if nxt:
                    for k in range(2):
                        ring_lo_part(R_IN + 2 * p, 4, i, 2 + k, ring_lo[:, k, :], ring_hi[:, k, :].bitcast(F32))
            steps(eng, in_step)
            for k in range(2 * KT):
                at = (slice(None), k // 2, slice(HALF * (k % 2), HALF * (k % 2 + 1)))
                ring_lo_part(R_CTX, 0, 0, k, ctx_lo[at], ctx_hi[at].bitcast(F32))
            for k in range(2):
                ring_lo_part(R_KV, 2, 0, k, ring_lo[:, k, :], ring_hi[:, k, :].bitcast(F32))

            def kv_step(i, p, nxt):
                if nxt:
                    for k in range(2):
                        ring_lo_part(R_KV + 2 * p, 4, i, 2 + k, ring_lo[:, k, :], ring_hi[:, k, :].bitcast(F32))

            def scan_prep_w(h, i, p):
                s = NC * h + 2 * i + p
                eng.wait_ge(wdt_hi_ok, s + 1)
                nc.gpsimd.tensor_tensor(B["wdt_lo"][:, :], B["wdt"][:, :], B["wdt_hi"][:, :].bitcast(F32),
                                        ALU.subtract).then_inc(wdt_ok, 1)

            def scan_prep_u(h, i, p):
                s = NC * h + 2 * i + p
                eng.wait_ge(dt_ok, s + 1)
                eng.wait_ge(ch_full[3], 2 * s)
                nc.gpsimd.tensor_tensor(B["dtu"][:, :], B["dt"][:, :], B["u"][:, p, :],
                                        ALU.mult).then_inc(dtu_ok, 1)

            def scan_step(h, i, p, nxt):
                s = NC * h + 2 * i + p
                eng.wait_ge(dtu_ok, s + 1)
                for j in range(CHUNKS):
                    slot = j % 4
                    eng.wait_ge(ch_free[slot], 2 * s + j // 4)
                    nc.gpsimd.tensor_tensor(
                        ch[:, slot, :].rearrange("p (n t) -> p n t", n=CH_N),
                        B["dtu"][:, None, :].broadcast_to([P, CH_N, HALF]),
                        B["bc"][:, CH_N * j:CH_N * (j + 1), :], ALU.mult).then_inc(ch_full[slot], 1)
                    if j == 1:
                        eng.wait_ge(wo_hi_ok, s + 1)
                        nc.gpsimd.tensor_tensor(B["wo_lo"][:, :], B["wo"][:, :], B["wo_hi"][:, :].bitcast(F32),
                                                ALU.subtract).then_inc(wo_ok, 1)
                        if nxt:
                            scan_prep_w(h, i + p, 1 - p)
                if nxt:
                    scan_prep_u(h, i + p, 1 - p)

            steps(eng, kv_step)
            for h in range(2):
                scan_prep_w(h, 0, 0)
                scan_prep_u(h, 0, 0)
                for k in range(2):
                    eng.wait_ge(s_free[k], (S_BC[h] + NS) // 2)
                    eng.wait_ge(d_free[k], (D_BC[h] + NS) // 2)
                steps(eng, lambda i, p, nxt: scan_step(h, i, p, nxt))

            def x_step(h, i, p, nxt):
                s = G * h + 2 * i + p
                for j in range(HPG):
                    ring_lo_part(R_X[h] + 2 * HPG * p, 4 * HPG, i, j, wd_lo[:, j, :], wd_hi[:, j, :].bitcast(F32))
                for b in range(NB):
                    eng.wait_ge(rcp_ok, NB * s + b + 1)
                    nc.gpsimd.tensor_tensor(pr[:, b % 2, :, :], pr[:, b % 2, :, :],
                                            rcp[:, b % 2, :, None].broadcast_to([P, HPG, P]),
                                            ALU.mult).then_inc(pn_ok, 1)
                    if nxt:
                        ring_lo_part(R_X[h] + 2 * HPG * p, 4 * HPG, i, HPG + b, ring_lo[:, b % 2, :],
                                     ring_hi[:, b % 2, :].bitcast(F32))

            for h in range(2):
                for j in range(HPG):
                    ring_lo_part(R_Q[h], 0, 0, j, ring_lo[:, j % 2, :], ring_hi[:, j % 2, :].bitcast(F32))
                steps(eng, lambda i, p, nxt: x_step(h, i, p, nxt))
            ring_lo_part(R_FFN, 0, 0, 0, r_lo[:, :], r_hi[:, :].bitcast(F32))
            for k in range(KT):
                ring_lo_part(R_FFN, 0, 0, 1 + k, a_lo[:, k, :], a_hi[:, k, :].bitcast(F32))
            for k in range(KT):
                ring_lo_part(R_FFN, 0, 0, 1 + KT + k, b_lo[:, k, :], b_hi[:, k, :].bitcast(F32))

        @block.scalar
        def _(eng):
            act = nc.scalar.activation

            def ring_hi_part(base, per, i, k, hi):
                slot, n = use(base, per, i, k)
                eng.wait_ge(raw_in[slot], 16 * n + 16)
                act(hi, raw[:, slot, :], ACT.Copy).then_inc(w_hi_ok[slot], 1)

            def hl_part(base, per, i, k, hi):
                slot, n = use(base, per, i, k)
                eng.wait_ge(hl_full[slot], n + 1)
                act(hi, hl_bank[slot][:, :], ACT.Copy).then_inc(hl_hi[slot], 1)

            def ln_rstd_part(l):
                eng.wait_ge(ln_stat, l + 1)
                act(lnv[:, :], mv[:, :, 1], ACT.Ln, bias=eps_ln[:, :]).then_inc(ln_rstd, 1)
                eng.wait_ge(ln_rstd, 2 * l + 1)
                act(rstd[:, :], lnv[:, :], ACT.Exp, scale=-0.5).then_inc(ln_rstd, 1)

            eng.wait_ge(const_ok, 6)
            act(ident_r[:, :], ident[:, :], ACT.Copy).then_inc(masks_ok, 1)
            act(mask_r[:, :], mask[:, :], ACT.Copy).then_inc(masks_ok, 1)
            ring_hi_part(R_WX, 0, 0, 0, wx_hi[:, :])
            for k in range(2):
                ring_hi_part(R_IN, 2, 0, k, ring_hi[:, k, :])
            for h in range(2):
                ln_rstd_part(h)
                for k in range(KT):
                    hl_part(HL_LN1, 0, 0, KT * h + k, (xt_hi, xt1_hi)[h][:, k, :])
            eng.wait_ge(zero_ok, 1)

            def in_step(i, p, nxt):
                c = 2 * i + p
                for h in range(2):
                    slot, n = use(S_IN + 4 * p, 8, i, h)
                    eng.wait_ge(s_full[slot], n + 1)
                    eng.wait_ge(conv_ok, 2 * c)
                    act(xpad[:, h, :, TAPS - 1:], s_bank[slot][:, :].rearrange("p (b t) -> p b t", b=NB),
                        ACT.Copy).then_inc(s_free[slot], 1)
                if nxt:
                    ring_hi_part(R_IN + 2 * p, 4, i, 2, ring_hi[:, 0, :])
                for h in range(2):
                    slot, n = use(S_IN + 4 * p, 8, i, 2 + h)
                    eng.wait_ge(s_full[slot], n + 1)
                    if h == 0:
                        eng.wait_ge(spill[p], 64 * i)
                    act(sg_out[:, p, h, :], s_bank[slot][:, :], ACT.Silu).then_inc(gate_ok, 1)
                    eng.wait_ge(gate_ok, 2 * c + h + 1)
                    eng.sem_inc(s_free[slot], 1)
                if nxt:
                    ring_hi_part(R_IN + 2 * p, 4, i, 3, ring_hi[:, 1, :])
                for h in range(2):
                    eng.wait_ge(conv_ok, 2 * c + h + 1)
                    act(u_out[:, p, h, :], conv[:, h, :], ACT.Silu).then_inc(silu_ok, 1)
                    eng.wait_ge(silu_ok, 2 * c + h + 1)
                    eng.wait_ge(d_full[(D_IN + h) % 2], D_IN // 2 + c)
                    act(u_hi[:, h, :], u_out[:, p, h, :], ACT.Copy).then_inc(uhi_ok, 1)
            steps(eng, in_step)

            eng.wait_ge(ssm_ch, 4)
            act(ssm_ln[:, 0, :], ssm_ss[:, 0, :], ACT.Ln, bias=eps_rms[:, :], scale=1.0 / RDT).then_inc(ssm_rs_ok, 1)
            act(ssm_ln[:, 1:3, :], ssm_ss[:, 1:3, :], ACT.Ln, bias=eps_rms[:, :],
                scale=1.0 / NS).then_inc(ssm_rs_ok, 1)
            eng.wait_ge(ssm_rs_ok, 2)
            act(ssm_rs[:, :, :], ssm_ln[:, :, :], ACT.Exp, scale=-0.5).then_inc(ssm_rs_ok, 1)
            for h in range(2):
                slot, n = use(HL_SSM, 0, 0, h)
                eng.wait_ge(hl_full[slot], n + 1)
                act(stk[0:SSM, h, :], hl_bank[slot][0:SSM, :], ACT.Copy).then_inc(stk_cp, 1)
                if h:
                    eng.wait_ge(hl_free[use(HL_SSM, 0, 0, 0)[0]], use(HL_SSM, 0, 0, 0)[1] + 1)
                act(stk_t[SSM:P, :], hl_bank[slot][SSM:P, :], ACT.Copy).then_inc(hl_hi[slot], 1)
            for k in range(2):
                eng.wait_ge(spill[k], 64 * (NC // 2))
                eng.wait_ge(hl_free[k], HL_KV // 2)
            for k in range(2 * KT):
                ring_hi_part(R_CTX, 0, 0, k, ctx_hi[:, k // 2, HALF * (k % 2):HALF * (k % 2 + 1)])
            for k in range(2):
                ring_hi_part(R_KV, 2, 0, k, ring_hi[:, k, :])

            def kv_step(i, p, nxt):
                for k in range(4):
                    slot, n = use(HL_KV + 4 * p, 8, i, k)
                    eng.wait_ge(stg_out[slot], 32 * (n - HL_KV // 2))
                    hl_part(HL_KV + 4 * p, 8, i, k, stg_hi[:, slot, :])
                    if nxt and k % 2:
                        ring_hi_part(R_KV + 2 * p, 4, i, 2 + k // 2, ring_hi[:, k // 2, :])

            def scan_prep_w(h, i, p):
                s = NC * h + 2 * i + p
                eng.wait_ge(ws_in, 16 * s + 16)
                eng.wait_ge(dt_full, s)
                act(B["wdt_hi"][:, :], B["wdt"][:, :], ACT.Copy).then_inc(wdt_hi_ok, 1)

            def scan_prep(h, i, p, s_y):
                s, n = NC * h + 2 * i + p, (NC // 2) * h + i
                eng.wait_ge(scan_in[p], 32 * n + 32)
                eng.wait_ge(al_ok, s + 1)
                act(B["ea"][:, p, :], B["ea"][:, p, :], ACT.Exp).then_inc(ea_ok, 1)
                eng.wait_ge(dt_full, s + 1)
                eng.wait_ge(dt_ok, s)
                eng.wait_ge(ylo_ok, s_y)
                act(B["sp"][:, :], dt_bank[:, :], ACT.Abs, bias=cst_sb[:, p, DTB:DTB + 1]).then_inc(dt_abs, 1)
                eng.wait_ge(dt_abs, s + 1)
                act(B["sp"][:, :], B["sp"][:, :], ACT.Exp, scale=-1.0).then_inc(dt_exp, 1)
                eng.wait_ge(dt_exp, 2 * s + 1)
                act(B["y"][:, :], B["sp"][:, :], ACT.Identity, bias=1.0).then_inc(dt_exp, 1)

            def scan_prep_ln(h, i, p):
                s = NC * h + 2 * i + p
                eng.wait_ge(dt_err, s + 1)
                act(B["y"][:, :], B["y"][:, :], ACT.Ln).then_inc(dt_ln, 1)

            def scan_step(h, i, p, nxt):
                s = NC * h + 2 * i + p
                eng.wait_ge(dt_ok, s + 1)
                eng.wait_ge(na_ok, s + 1)
                for j in range(CHUNKS):
                    slot = j % 2
                    eng.wait_ge(scan_done[slot], 4 * s + j // 2)
                    for m in range(CH_N):
                        last = act(da[:, slot, m, :].rearrange("p (b t) -> p b t", b=NB)[:, :, 1:],
                                   B["dt"][:, :].rearrange("p (b t) -> p b t", b=NB)[:, :, 1:], ACT.Exp,
                                   scale=B["na"][:, p, CH_N * j + m:CH_N * j + m + 1])
                    last.then_inc(da_full[slot], 1)
                    if j == 0:
                        eng.wait_ge(sg_in, 32 * s + 32)
                        for k in range(2):
                            eng.wait_ge(d_full[k], D_SCAN[h] // 2 + (NB // 2) * (2 * i + p))
                        act(B["wo_hi"][:, :], B["wo"][:, :], ACT.Copy).then_inc(wo_hi_ok, 1)
                        if nxt:
                            scan_prep_w(h, i + p, 1 - p)
                    if j == 4 and nxt:
                        scan_prep(h, i + p, 1 - p, s)
                if nxt:
                    scan_prep_ln(h, i + p, 1 - p)
                eng.wait_ge(y_ok, s + 1)
                act(B["y_hi"][:, :], B["y"][:, :], ACT.Copy).then_inc(yhi_ok, 1)

            steps(eng, kv_step)
            for h in range(2):
                for k in range(NS):
                    slot, n = use(S_BC[h], 0, 0, k)
                    eng.wait_ge(s_full[slot], n + 1)
                    if h:
                        eng.wait_ge(ch_free[3], 2 * NC)
                    act(B["bc"][:, 2 * k, :], s_bank[slot][:, :], ACT.Copy).then_inc(s_free[slot], 1)
                scan_prep_w(h, 0, 0)
                scan_prep(h, 0, 0, NC * h)
                scan_prep_ln(h, 0, 0)
                steps(eng, lambda i, p, nxt: scan_step(h, i, p, nxt))

            def x_step(h, i, p, nxt):
                s = G * h + 2 * i + p
                for j in range(HPG):
                    if j == 0:
                        for k in range(2):
                            eng.wait_ge(d_full[k], D_X[h] // 2 + (NB // 2) * (2 * i + p))
                    ring_hi_part(R_X[h] + 2 * HPG * p, 4 * HPG, i, j, wd_hi[:, j, :])

                def probs(b):
                    slot, n = use(S_X[h] + NB * p, 2 * NB, i, b)
                    eng.wait_ge(mx_ok, NB * s + b + 1)
                    if b >= 2:
                        sl, m = use(HL_X[h] + XSTEP * p, 2 * XSTEP, i, PT_AT[nxt][b - 2])
                        eng.wait_ge(hl_full[sl], m + 1)
                    for j in range(HPG):
                        last = act(pr[:, b % 2, j, :], s_bank[slot][:, P * j:P * (j + 1)], ACT.Exp,
                                   bias=nmx[:, b % 2, j:j + 1], scale=DK ** -0.5,
                                   accum_out=psum_row[:, b % 2, j:j + 1])
                    last.then_inc(sum_ok, 1)

                def hl(k, hi):
                    hl_part(HL_X[h] + XSTEP * p, 2 * XSTEP, i, k, hi)

                probs(0)
                for b in range(NB):
                    if b + 1 < NB:
                        probs(b + 1)
                    hl(PT_AT[nxt][b], pt_hi[:, :])
                    if nxt and b >= 2:
                        hl(Q_AT[b - 2], q_hi[:, b - 2, :])
                        ring_hi_part(R_X[h] + 2 * HPG * p, 4 * HPG, i, HPG + b, ring_hi[:, b % 2, :])
                    if b >= 2:
                        sl, m = use(D_X[h] + NB * p, 2 * NB, i, b - 2)
                        eng.wait_ge(d_full[sl], m + 1)
                    hl(AT_AT[nxt][b], at_hi[:, b % 2, :])
                    if nxt and b < 2:
                        ring_hi_part(R_X[h] + 2 * HPG * p, 4 * HPG, i, HPG + b, ring_hi[:, b % 2, :])
                if nxt:
                    hl(Q_AT[2], q_hi[:, 2, :])
                    hl(Q_AT[3], q_hi[:, 3, :])

            for h in range(2):
                ln_rstd_part(2 + h)
                for k in range(KT):
                    hl_part(HL_LN2[h], 0, 0, k, xt_hi[:, k, :])
                if h == 0:
                    for k in range(2):
                        eng.wait_ge(stg_out[k], 32 * 2 * G)
                for j in range(HPG):
                    ring_hi_part(R_Q[h], 0, 0, j, ring_hi[:, j % 2, :])
                    hl_part(HL_Q[h], 0, 0, j, q_hi[:, j, :])
                steps(eng, lambda i, p, nxt: x_step(h, i, p, nxt))

            for k in range(2):
                eng.wait_ge(d_free[k], D_FFN // 2)
            for l in range(1 + 2 * KT):
                dst = r_hi[:, :] if l == 0 else a_hi[:, l - 1, :] if l <= KT else b_hi[:, l - 1 - KT, :]
                ring_hi_part(R_FFN, 0, 0, l, dst)
            for h in range(2):
                ln_rstd_part(4 + h)
                for k in range(KT):
                    hl_part(HL_LN3[h], 0, 0, k, xt_hi[:, k, :])
                slot, n = use(S_FFN, 0, 0, h)
                eng.wait_ge(s_full[slot], n + 1)
                act(qr[:, :], s_bank[slot][:, :], ACT.Copy).then_inc(s_free[slot], 1)
                eng.wait_ge(gate_f, h + 1)
                for t in range(NB):
                    last = act(ge[:, t, :], sco[:, t, :], ACT.Exp, bias=ntop[:, t:t + 1])
                last.then_inc(ge_ok, 1)
                for k in range(KT):
                    hl_part(HL_ZT[h], 0, 0, k, zt_hi[:, k, :])

        @block.vector
        def _(eng):
            def lo_part(base, per, i, k, lo, hi):
                slot, n = use(base, per, i, k)
                eng.wait_ge(hl_hi[slot], n + 1)
                nc.vector.tensor_tensor(lo, hl_bank[slot][:, :], hi.bitcast(F32), ALU.subtract).then_inc(
                    hl_free[slot], 1)

            def layer_norm(l, h):
                for t in range(NB):
                    nc.vector.bn_stats(stats[:, t, :], xres[:, NB * h + t, :]).then_inc(ln_mv, 1)
                eng.wait_ge(ln_mv, 2 * NB * l + NB)
                for t in range(NB):
                    last = nc.vector.bn_aggr(mv[:, t, :], stats[:, t, :]).then_inc(ln_mv, 1)
                eng.wait_ge(ln_mv, 2 * NB * l + 2 * NB)
                eng.sem_inc(ln_stat, 1)
                eng.wait_ge(ln_rstd, 2 * l + 2)
                for t in range(NB):
                    nc.vector.tensor_scalar(xn[:, t, :], xres[:, NB * h + t, :], mv[:, t, 0:1], rstd[:, t:t + 1],
                                            ALU.subtract, ALU.mult).then_inc(ln_xn, 1)

            nc.vector.memset(xpad[:, :, :, 0:TAPS - 1], 0.0).then_inc(zero_ok, 1)
            nc.vector.memset(ssm[:, :, :], 0.0).then_inc(zero_ok, 1)
            for h in range(2):
                eng.wait_ge(x_in[h], 16)
                if h:
                    for k in range(2):
                        eng.wait_ge(hl_full[k], KT // 2)
                layer_norm(h, h)
                for k in range(KT):
                    lo_part(HL_LN1, 0, 0, KT * h + k, (xt_lo, xt1_lo)[h][:, k, :], (xt_hi, xt1_hi)[h][:, k, :])
            nc.vector.memset(da[:, :, :, :], 0.0).then_inc(zero_ok, 1)
            eng.wait_ge(zero_ok, 3)

            def in_step(i, p, nxt):
                c = 2 * i + p
                conv_c = Chain(eng, conv_ch, 6, c)
                eng.wait_ge(cst_in[p], 16 * i + 16)
                for h in range(2):
                    slot, n = use(S_IN + 4 * p, 8, i, h)
                    eng.wait_ge(s_free[slot], n + 1)
                    eng.wait_ge(silu_ok, 2 * c)
                    rows = conv[:, h, :].rearrange("p (b t) -> p b t", b=NB)
                    conv_c.did(nc.vector.tensor_scalar(rows, xpad[:, h, :, 0:SEQ], cst_sb[:, p, CONV0:CONV0 + 1],
                                                       cst_sb[:, p, CONVB:CONVB + 1], ALU.mult, ALU.add))
                    for j in range(1, TAPS):
                        conv_c.wait()
                        ins = nc.vector.scalar_tensor_tensor(
                            out=rows, in0=xpad[:, h, :, j:j + SEQ], scalar=cst_sb[:, p, CONV0 + j:CONV0 + j + 1],
                            in1=rows, op0=ALU.mult, op1=ALU.add)
                        if j < TAPS - 1:
                            conv_c.did(ins)
                        else:
                            ins.then_inc(conv_ok, 1)
                conv_c.end()
                for h in range(2):
                    eng.wait_ge(uhi_ok, 2 * c + h + 1)
                    nc.vector.tensor_tensor(u_lo[:, h, :], u_out[:, p, h, :], u_hi[:, h, :].bitcast(F32),
                                            ALU.subtract).then_inc(ulo_ok, 1)
                for h in range(2):
                    slot, n = use(D_IN + 2 * p, 4, i, h)
                    eng.wait_ge(d_full[slot], n + 1)
                    eng.wait_ge(d_free[slot], n)
                    part = ssm[:, NB * h:NB * (h + 1), :].rearrange("p t n -> p (t n)")
                    nc.vector.tensor_tensor(part, part, d_bank[slot][:, 0:NB * SSM], ALU.add).then_inc(
                        d_free[slot], 1)
            steps(eng, in_step)

            for k in range(2):
                eng.wait_ge(d_free[k], (D_IN + 2 * NC) // 2)
            nc.vector.tensor_tensor(ssm_sq[:, :, :], ssm[:, :, :], ssm[:, :, :], ALU.mult).then_inc(ssm_ch, 1)
            eng.wait_ge(ssm_ch, 1)
            parts = [slice(0, RDT), slice(RDT, RDT + NS), slice(RDT + NS, SSM)]
            for k, cols in enumerate(parts):
                nc.vector.tensor_reduce(ssm_ss[:, k, :], ssm_sq[:, :, cols], AX_X, ALU.add).then_inc(ssm_ch, 1)
            eng.wait_ge(ssm_rs_ok, 3)
            for r in range(2):
                for k, cols in enumerate(parts):
                    n = cols.stop - cols.start
                    nc.vector.tensor_tensor(ssm_n[:, :, r, cols], ssm[:, :, cols],
                                            ssm_rs[:, k, :, None].broadcast_to([P, 2 * NB, n]),
                                            ALU.mult).then_inc(ssm_ch, 1)
            for h in range(2):
                slot, n = use(HL_SSM, 0, 0, h)
                eng.wait_ge(hl_hi[slot], n + 1)
                nc.vector.tensor_tensor(stk[SSM:P, h, :], hl_bank[slot][SSM:P, :], stk_t[SSM:P, :].bitcast(F32),
                                        ALU.subtract).then_inc(hl_free[slot], 1)
            for k in range(2):
                eng.wait_ge(spill[k], 64 * (NC // 2))
                eng.wait_ge(hl_free[k], HL_KV // 2)
            eng.wait_ge(const_ok, 6)
            nc.vector.tensor_tensor(sel_c[:, :], ident[:, RDT:SSM], ident[:, SSM + RDT:P], ALU.add).then_inc(
                sel_ok, 1)
            eng.wait_ge(sel_ok, 1)
            nc.vector.tensor_copy(sel[:, :, :], sel_c[:, :, None].broadcast_to([P, 2 * NS, P])).then_inc(sel_ok, 1)

            def kv_step(i, p, nxt):
                for k in range(4):
                    slot, n = use(HL_KV + 4 * p, 8, i, k)
                    eng.wait_ge(stg_out[slot], 32 * (n - HL_KV // 2))
                    lo_part(HL_KV + 4 * p, 8, i, k, stg_lo[:, slot, :], stg_hi[:, slot, :])

            def scan_prep(h, i, p):
                s = NC * h + 2 * i + p
                eng.wait_ge(ea_ok, s + 1)
                nc.vector.tensor_scalar(B["na"][:, p, :], B["ea"][:, p, :], -1.0, None, ALU.mult).then_inc(na_ok, 1)
                eng.wait_ge(dt_abs, s + 1)
                nc.vector.tensor_scalar(B["rl"][:, :], dt_bank[:, :], cst_sb[:, p, DTB:DTB + 1], 0.0,
                                        ALU.add, ALU.max).then_inc(dt_free, 1)
                eng.wait_ge(dt_exp, 2 * s + 2)
                nc.vector.scalar_tensor_tensor(out=B["sp"][:, :], in0=B["y"][:, :], scalar=1.0, in1=B["sp"][:, :],
                                               op0=ALU.subtract, op1=ALU.subtract).then_inc(dt_err, 1)
                eng.wait_ge(dt_free, s + 1)
                eng.wait_ge(dt_err, s + 1)
                nc.vector.tensor_tensor(B["rl"][:, :], B["rl"][:, :], B["sp"][:, :], ALU.subtract).then_inc(
                    dt_rest, 1)

            def scan_prep_dt(h, i, p):
                s = NC * h + 2 * i + p
                eng.wait_ge(dt_rest, s + 1)
                eng.wait_ge(dt_ln, s + 1)
                nc.vector.tensor_tensor(B["dt"][:, :], B["rl"][:, :], B["y"][:, :], ALU.add).then_inc(dt_ok, 1)

            def scan_prep_a(h, i, p):
                n = (NC // 2) * h + i
                eng.wait_ge(scan_in[p], 32 * n + 32)
                nc.vector.tensor_scalar(B["ea"][:, p, :], cst_sb[:, p, 0:NS], A_LOG_MAX, None, ALU.min).then_inc(
                    al_ok, 1)

            def scan_step(h, i, p, nxt):
                s = NC * h + 2 * i + p

                def scan(j):
                    slot, cs = j % 2, j % 4
                    eng.wait_ge(da_full[slot], 4 * s + j // 2 + 1)
                    eng.wait_ge(ch_full[cs], 2 * s + j // 4 + 1)
                    nc.vector.tensor_tensor_scan(
                        ch[:, cs, :], da[:, slot, :, :].rearrange("p n t -> p (n t)"), ch[:, cs, :], 0.0,
                        ALU.mult, ALU.add).then_inc(scan_done[slot], 1)

                def times_c(j):
                    slot, cs = j % 2, j % 4
                    eng.wait_ge(scan_done[slot], 4 * s + j // 2 + 1)
                    nc.vector.tensor_tensor(
                        ch[:, cs, :], ch[:, cs, :],
                        B["bc"][:, NS + CH_N * j:NS + CH_N * (j + 1), :].rearrange("p n t -> p (n t)"),
                        ALU.mult).then_inc(ch_mul[cs], 1)

                scan(0)
                for j in range(1, CHUNKS):
                    scan(j)
                    times_c(j - 1)
                    if j == 1 and nxt:
                        scan_prep_a(h, i + p, 1 - p)
                    if j == 6 and nxt:
                        scan_prep(h, i + p, 1 - p)
                times_c(CHUNKS - 1)
                if nxt:
                    scan_prep_dt(h, i + p, 1 - p)
                eng.wait_ge(y_full, s + 1)
                eng.wait_ge(sg_in, 32 * s + 32)
                eng.wait_ge(yhi_ok, s)
                eng.wait_ge(ylo_ok, s)
                eng.wait_ge(dt_ok, s + (2 if nxt else 1))
                nc.vector.scalar_tensor_tensor(out=B["y"][:, :], in0=B["u"][:, p, :],
                                               scalar=cst_sb[:, p, DSKIP:DSKIP + 1], in1=y_bank[:, :],
                                               op0=ALU.mult, op1=ALU.add).then_inc(y_free, 1)
                eng.wait_ge(y_free, s + 1)
                nc.vector.tensor_tensor(B["y"][:, :], B["y"][:, :], B["sg"][:, :], ALU.mult).then_inc(y_ok, 1)
                eng.wait_ge(yhi_ok, s + 1)
                nc.vector.tensor_tensor(B["y_lo"][:, :], B["y"][:, :], B["y_hi"][:, :].bitcast(F32),
                                        ALU.subtract).then_inc(ylo_ok, 1)
                for t in range(NB):
                    add_to_x(D_SCAN[h] + NB * p, 2 * NB, i, t, NB * h + t)

            def add_to_x(base, per, i, k, t):
                slot, n = use(base, per, i, k)
                eng.wait_ge(d_full[slot], n + 1)
                eng.wait_ge(d_free[slot], n - 1)
                nc.vector.tensor_tensor(xres[:, t, :], xres[:, t, :], d_bank[slot][:, :], ALU.add).then_inc(
                    d_free[slot], 1)

            steps(eng, kv_step)
            for h in range(2):
                for k in range(NS):
                    slot, n = use(D_BC[h], 0, 0, k)
                    eng.wait_ge(d_full[slot], n + 1)
                    nc.vector.tensor_copy(B["bc"][:, 2 * k + 1, :], d_bank[slot][:, :]).then_inc(d_free[slot], 1)
                scan_prep_a(h, 0, 0)
                scan_prep(h, 0, 0)
                scan_prep_dt(h, 0, 0)
                for k in range(2):
                    eng.wait_ge(s_free[k], (S_BC[h] + NS) // 2)
                    eng.wait_ge(d_free[k], (D_BC[h] + NS) // 2)
                steps(eng, lambda i, p, nxt: scan_step(h, i, p, nxt))

            def x_step(h, i, p, nxt):
                s = G * h + 2 * i + p

                def row_max(b):
                    slot, n = use(S_X[h] + NB * p, 2 * NB, i, b)
                    eng.wait_ge(s_full[slot], n + 1)
                    nc.vector.tensor_reduce(mx[:, b % 2, :], s_bank[slot][:, :].rearrange("p (h k) -> p h k", h=HPG),
                                            AX_X, ALU.max).then_inc(mx_ch, 1)
                    eng.wait_ge(mx_ch, NB * s + b + 1)
                    nc.vector.tensor_scalar(nmx[:, b % 2, :], mx[:, b % 2, :], -DK ** -0.5, None,
                                            ALU.mult).then_inc(mx_ok, 1)

                def recip(b):
                    slot, n = use(S_X[h] + NB * p, 2 * NB, i, b)
                    eng.wait_ge(sum_ok, NB * s + b + 1)
                    nc.vector.reciprocal(rcp[:, b % 2, :], psum_row[:, b % 2, :]).then_inc(rcp_ok, 1)
                    eng.sem_inc(s_free[slot], 1)

                def lo(k, lo_, hi_):
                    lo_part(HL_X[h] + XSTEP * p, 2 * XSTEP, i, k, lo_, hi_)

                def x_add(b):
                    add_to_x(D_X[h] + NB * p, 2 * NB, i, b, NB * h + b)

                row_max(0)
                row_max(1)
                recip(0)
                for b in range(NB):
                    if b + 1 < NB:
                        recip(b + 1)
                    lo(PT_AT[nxt][b], pt_lo[:, :], pt_hi[:, :])
                    if b + 2 < NB:
                        row_max(b + 2)
                    elif nxt:
                        lo(Q_AT[b - 2], q_lo[:, b - 2, :], q_hi[:, b - 2, :])
                    lo(AT_AT[nxt][b], at_lo[:, b % 2, :], at_hi[:, b % 2, :])
                    if b:
                        x_add(b - 1)
                if nxt:
                    lo(Q_AT[2], q_lo[:, 2, :], q_hi[:, 2, :])
                x_add(NB - 1)
                if nxt:
                    lo(Q_AT[3], q_lo[:, 3, :], q_hi[:, 3, :])

            for h in range(2):
                for k in range(2):
                    eng.wait_ge(d_free[k], D_X[h] // 2)
                    eng.wait_ge(ch_free[k], 2 * 2 * NC)
                if h:
                    for k in range(2):
                        eng.wait_ge(hl_full[k], HL_LN2[h] // 2)
                layer_norm(2 + h, h)
                for k in range(KT):
                    lo_part(HL_LN2[h], 0, 0, k, xt_lo[:, k, :], xt_hi[:, k, :])
                if h == 0:
                    for k in range(2):
                        eng.wait_ge(stg_out[k], 32 * 2 * G)
                for j in range(HPG):
                    lo_part(HL_Q[h], 0, 0, j, q_lo[:, j, :], q_hi[:, j, :])
                steps(eng, lambda i, p, nxt: x_step(h, i, p, nxt))

            for k in range(2):
                eng.wait_ge(d_free[k], D_FFN // 2)
            for h in range(2):
                f = Chain(eng, ffn_ch, 6 * NB + 3, h)
                if h:
                    for k in range(2):
                        eng.wait_ge(hl_full[k], HL_LN3[h] // 2)
                layer_norm(4 + h, h)
                for k in range(KT):
                    lo_part(HL_LN3[h], 0, 0, k, xt_lo[:, k, :], xt_hi[:, k, :])
                slot, n = use(D_FFN, 0, 0, (2 * NB + 1) * h)
                eng.wait_ge(d_full[slot], n + 1)
                if h:
                    eng.wait_ge(ge_ok, h)
                nc.vector.tensor_copy(sco[:, :, :].rearrange("p t e -> p (t e)"),
                                      d_bank[slot][:, 0:NB * EXPERTS]).then_inc(d_free[slot], 1)
                eng.wait_ge(d_free[slot], n + 1)
                for t in range(NB):
                    f.did(nc.vector.max(out=top[:, t, 0, :], in_=sco[:, t, :]))
                f.wait()
                nc.vector.tensor_scalar(ntop[:, :], top[:, :, 0, 0], -1.0, None, ALU.mult).then_inc(gate_f, 1)
                for t in range(NB):
                    f.did(nc.vector.match_replace(out=sco1[:, t, :], in_to_replace=top[:, t, 0, :],
                                                  in_values=sco[:, t, :], imm_value=NEG))
                f.wait()
                for t in range(NB):
                    f.did(nc.vector.max(out=top[:, t, 1, :], in_=sco1[:, t, :]))
                f.wait()
                for t in range(NB):
                    f.did(nc.vector.match_replace(out=sco2[:, t, :], in_to_replace=top[:, t, 1, :],
                                                  in_values=sco1[:, t, :], imm_value=NEG))
                f.wait()
                f.did(nc.vector.tensor_scalar(picked[:, :, :], sco2[:, :, :], NEG, None, ALU.is_equal))
                f.wait()
                eng.wait_ge(ge_ok, h + 1)
                f.did(nc.vector.tensor_tensor(picked[:, :, :], picked[:, :, :], ge[:, :, :], ALU.mult))
                f.wait()
                f.did(nc.vector.tensor_reduce(gsum[:, :], picked[:, :, :], AX_X, ALU.add))
                f.wait()
                for t in range(NB):
                    f.did(nc.vector.reciprocal(grcp[:, t:t + 1], gsum[:, t:t + 1]))
                f.wait()
                for t in range(NB):
                    f.did(nc.vector.tensor_scalar(picked[:, t, :], picked[:, t, :], grcp[:, t:t + 1], None, ALU.mult))
                f.wait()
                f.end()
                if h:
                    for k in range(2):
                        eng.wait_ge(hl_full[k], HL_LN3[h] // 2)
                for t in range(NB):
                    slot, n = use(D_FFN, 0, 0, (2 * NB + 1) * h + 1 + t)
                    eng.wait_ge(d_full[slot], n + 1)
                    nc.vector.tensor_tensor(zg[:, t, :].rearrange("p (e r) -> p e r", r=RANK),
                                            d_bank[slot][:, :].rearrange("p (e r) -> p e r", r=RANK),
                                            picked[:, t, :, None].broadcast_to([P, EXPERTS, RANK]),
                                            ALU.mult).then_inc(d_free[slot], 1)
                for k in range(KT):
                    lo_part(HL_ZT[h], 0, 0, k, zt_lo[:, k, :], zt_hi[:, k, :])
                for t in range(NB):
                    slot, n = use(D_FFN, 0, 0, (2 * NB + 1) * h + 1 + NB + t)
                    eng.wait_ge(d_full[slot], n + 1)
                    nc.vector.scalar_tensor_tensor(out=res[:, NB * h + t, :], in0=d_bank[slot][:, :], scalar=2.0,
                                                   in1=xres[:, NB * h + t, :], op0=ALU.mult,
                                                   op1=ALU.add).then_inc(out_ok, 1)
                    eng.wait_ge(out_ok, NB * h + t + 1)
                    eng.sem_inc(d_free[slot], 1)

        @block.tensor
        def _(eng):
            mm = nc.tensor.matmul

            def begin(kind_free, base, per, i, k):
                slot, n = use(base, per, i, k)
                eng.wait_ge(kind_free[slot], n)
                return slot

            def three(dst, w_hi, w_lo, m_hi, m_lo, first, last):
                mm(dst, w_hi, m_hi, start=first, stop=False)
                mm(dst, w_lo, m_hi, start=False, stop=False)
                return mm(dst, w_hi, m_lo, start=False, stop=last)

            def over_k(dst, w, m):
                for k in range(KT):
                    ins = three(dst, w[0](k), w[1](k), m[0](k), m[1](k), k == 0, k == KT - 1)
                return ins

            def transposes(slot, src):
                for t in range(NB):
                    ins = nc.tensor.transpose(hl_bank[slot][:, P * t:P * (t + 1)], src(t), ident[:, :])
                ins.then_inc(hl_full[slot], 1)

            def layer_norm(l, base, k0):
                eng.wait_ge(ln_xn, NB * l + NB)
                for k in range(KT):
                    slot = begin(hl_free, base, 0, 0, k0 + k)
                    transposes(slot, lambda t: xn[:, t, P * k:P * (k + 1)])

            def ring(slot):
                return (lambda k: ring_hi[:, slot, P * k:P * (k + 1)]), (lambda k: ring_lo[:, slot, P * k:P * (k + 1)])

            def ring_ready(base, per, i, k):
                slot, n = use(base, per, i, k)
                eng.wait_ge(w_ok[slot], n + 1)

            eng.wait_ge(const_ok, 6)
            for h in range(2):
                layer_norm(h, HL_LN1, KT * h)
            for k in range(2):
                eng.wait_ge(hl_free[k], (HL_LN1 + 2 * KT) // 2)
            ring_ready(R_WX, 0, 0, 0)
            xts = [((lambda k: xt_hi[:, k, :]), (lambda k: xt_lo[:, k, :])),
                   ((lambda k: xt1_hi[:, k, :]), (lambda k: xt1_lo[:, k, :]))]

            def in_step(i, p, nxt):
                c = 2 * i + p
                for part in range(2):
                    ring_ready(R_IN + 2 * p, 4, i, part)
                    for h in range(2):
                        slot = begin(s_free, S_IN + 4 * p, 8, i, 2 * part + h)
                        over_k(s_bank[slot][:, :], ring(part), xts[h]).then_inc(s_full[slot], 1)
                for h in range(2):
                    slot = begin(d_free, D_IN + 2 * p, 4, i, h)
                    eng.wait_ge(ulo_ok, 2 * c + h + 1)
                    for t in range(NB):
                        rows = slice(P * t, P * (t + 1))
                        ins = three(d_bank[slot][:, SSM * t:SSM * (t + 1)], u_hi[:, h, rows], u_lo[:, h, rows],
                                    wx_hi[:, bass.ds(SSM * c, SSM)], wx_lo[:, bass.ds(SSM * c, SSM)], True, True)
                    ins.then_inc(d_full[slot], 1)
            steps(eng, in_step)

            eng.wait_ge(ssm_ch, 4 + 6)
            for h in range(2):
                slot = begin(hl_free, HL_SSM, 0, 0, h)
                transposes(slot, lambda t: ssm_n[:, NB * h + t, :, :].rearrange("p a n -> p (a n)"))
            for k in range(2):
                eng.wait_ge(w_ok[(R_CTX + k) % 2], (R_CTX + 2 * KT + k) // 2)

            def kv_step(i, p, nxt):
                for k in range(4):
                    part, h = k // 2, k % 2
                    if h == 0:
                        ring_ready(R_KV + 2 * p, 4, i, part)
                    slot = begin(hl_free, HL_KV + 4 * p, 8, i, k)
                    if part == 0:
                        ins = over_k(hl_bank[slot][:, :], ring(0),
                                     ((lambda q: ctx_hi[:, q, HALF * h:HALF * (h + 1)]),
                                      (lambda q: ctx_lo[:, q, HALF * h:HALF * (h + 1)])))
                    else:
                        for t in range(NB):
                            rows = slice(HALF * h + P * t, HALF * h + P * (t + 1))
                            ins = over_k(hl_bank[slot][:, DK * t:DK * (t + 1)],
                                         ((lambda q: ctx_hi[:, q, rows]), (lambda q: ctx_lo[:, q, rows])), ring(1))
                    ins.then_inc(hl_full[slot], 1)

            def scan_prep(h, i, p):
                s = NC * h + 2 * i + p
                eng.wait_ge(wdt_ok, s + 1)
                eng.wait_ge(dt_free, s)
                mm(dt_bank[:, :], B["wdt_hi"][:, :], stk[:, h, :], start=True, stop=False)
                mm(dt_bank[:, :], B["wdt_lo"][:, :], stk[:, h, :], start=False, stop=True).then_inc(dt_full, 1)

            def scan_step(h, i, p, nxt):
                s = NC * h + 2 * i + p
                eng.wait_ge(y_free, s)
                for j in range(CHUNKS):
                    cs = j % 4
                    eng.wait_ge(ch_mul[cs], 2 * s + j // 4 + 1)
                    for m in range(CH_N):
                        ins = mm(y_bank[:, :], ident[:, :], ch[:, cs, HALF * m:HALF * (m + 1)],
                                 start=(j == 0 and m == 0), stop=(j == CHUNKS - 1 and m == CH_N - 1))
                    ins.then_inc(ch_free[cs], 1)
                    if j == 1 and nxt:
                        scan_prep(h, i + p, 1 - p)
                    if j == CHUNKS - 1:
                        eng.wait_ge(ch_free[cs], 2 * s + 2)
                        eng.sem_inc(y_full, 1)
                eng.wait_ge(wo_ok, s + 1)
                eng.wait_ge(ylo_ok, s + 1)
                for t in range(NB):
                    slot = begin(d_free, D_SCAN[h] + NB * p, 2 * NB, i, t)
                    rows = slice(P * t, P * (t + 1))
                    three(d_bank[slot][:, :], B["y_hi"][:, rows], B["y_lo"][:, rows], B["wo_hi"][:, :],
                          B["wo_lo"][:, :], True, True).then_inc(d_full[slot], 1)

            steps(eng, kv_step)
            eng.wait_ge(sel_ok, 2)
            for h in range(2):
                for k in range(NS):
                    slot = begin(s_free, S_BC[h], 0, 0, k)
                    mm(s_bank[slot][:, :], sel[:, 2 * k, :], stk[:, h, :], start=True, stop=True).then_inc(
                        s_full[slot], 1)
                    slot = begin(d_free, D_BC[h], 0, 0, k)
                    mm(d_bank[slot][:, :], sel[:, 2 * k + 1, :], stk[:, h, :], start=True, stop=True).then_inc(
                        d_full[slot], 1)
                scan_prep(h, 0, 0)
                steps(eng, lambda i, p, nxt: scan_step(h, i, p, nxt))

            def project_q(base, per, i, k, rbase, rper, rk, j):
                ring_ready(rbase, rper, i, rk)
                slot = begin(hl_free, base, per, i, k)
                over_k(hl_bank[slot][:, :], ring(j % 2), xts[0]).then_inc(hl_full[slot], 1)

            def x_step(h, i, p, nxt):
                s = G * h + 2 * i + p
                hb, hper = HL_X[h] + XSTEP * p, 2 * XSTEP

                def scores(b):
                    slot = begin(s_free, S_X[h] + NB * p, 2 * NB, i, b)
                    rows = slice(P * b, P * (b + 1))
                    mm(s_bank[slot][:, :].rearrange("p (h k) -> p h k", h=HPG), ident_r[:, :],
                       mask_r[:, None, :].broadcast_to([P, HPG, P]), start=True, stop=False)
                    for j in range(HPG):
                        ins = three(s_bank[slot][:, P * j:P * (j + 1)], q_hi[:, j, rows], q_lo[:, j, rows],
                                    kv[:, 0, 0, rows], kv[:, 0, 1, rows], False, j == HPG - 1)
                    ins.then_inc(s_full[slot], 1)

                def turn(b):
                    eng.wait_ge(pn_ok, NB * s + b + 1)
                    slot = begin(hl_free, hb, hper, i, PT_AT[nxt][b])
                    transposes(slot, lambda j: pr[:, b % 2, j, :])

                def attend(b):
                    sl, n = use(hb, hper, i, PT_AT[nxt][b])
                    eng.wait_ge(hl_free[sl], n + 1)
                    slot = begin(hl_free, hb, hper, i, AT_AT[nxt][b])
                    rows = slice(P * b, P * (b + 1))
                    three(hl_bank[slot][:, :], kv[:, 1, 0, rows], kv[:, 1, 1, rows], pt_hi[:, :], pt_lo[:, :],
                          True, True).then_inc(hl_full[slot], 1)

                def project_out(b):
                    sl, n = use(hb, hper, i, AT_AT[nxt][b])
                    eng.wait_ge(hl_free[sl], n + 1)
                    if b == 0:
                        for j in range(HPG):
                            ring_ready(R_X[h] + 2 * HPG * p, 4 * HPG, i, j)
                    slot = begin(d_free, D_X[h] + NB * p, 2 * NB, i, b)
                    for j in range(HPG):
                        cols = slice(P * j, P * (j + 1))
                        ins = three(d_bank[slot][:, :], at_hi[:, b % 2, cols], at_lo[:, b % 2, cols],
                                    wd_hi[:, j, :], wd_lo[:, j, :], j == 0, j == HPG - 1)
                    ins.then_inc(d_full[slot], 1)

                def next_q(j):
                    if nxt:
                        project_q(hb, hper, i, Q_AT[j], R_X[h] + 2 * HPG * p, 4 * HPG, HPG + j, j)

                eng.wait_ge(kv_in, 64 * s + 64)
                for k in range(2):
                    eng.wait_ge(hl_free[k], hb // 2 + XSTEP * i)
                scores(0)
                scores(1)
                turn(0)
                scores(2)
                attend(0)
                turn(1)
                project_out(0)
                scores(3)
                attend(1)
                turn(2)
                project_out(1)
                next_q(0)
                attend(2)
                turn(3)
                project_out(2)
                next_q(1)
                attend(3)
                next_q(2)
                project_out(3)
                next_q(3)

            for h in range(2):
                layer_norm(2 + h, HL_LN2[h], 0)
                for k in range(2):
                    eng.wait_ge(hl_free[k], HL_Q[h] // 2)
                for j in range(HPG):
                    project_q(HL_Q[h], 0, 0, j, R_Q[h], 0, j, j)
                for k in range(2):
                    eng.wait_ge(hl_free[k], HL_X[h] // 2)
                steps(eng, lambda i, p, nxt: x_step(h, i, p, nxt))

            for h in range(2):
                layer_norm(4 + h, HL_LN3[h], 0)
                for k in range(2):
                    eng.wait_ge(hl_free[k], HL_ZT[h] // 2)
                ring_ready(R_FFN, 0, 0, 0)
                slot = begin(s_free, S_FFN, 0, 0, h)
                over_k(s_bank[slot][:, :], ((lambda k: r_hi[:, P * k:P * (k + 1)]),
                                            (lambda k: r_lo[:, P * k:P * (k + 1)])), xts[0]).then_inc(s_full[slot], 1)
                eng.wait_ge(keys_in, 16)
                eng.wait_ge(s_free[slot], use(S_FFN, 0, 0, h)[1] + 1)
                slot = begin(d_free, D_FFN, 0, 0, (2 * NB + 1) * h)
                for t in range(NB):
                    ins = mm(d_bank[slot][:, EXPERTS * t:EXPERTS * (t + 1)], qr[:, P * t:P * (t + 1)], keys_sb[:, :],
                             start=True, stop=True)
                ins.then_inc(d_full[slot], 1)
                for k in range(KT):
                    ring_ready(R_FFN, 0, 0, 1 + k)
                for t in range(NB):
                    slot = begin(d_free, D_FFN, 0, 0, (2 * NB + 1) * h + 1 + t)
                    rows = slice(P * t, P * (t + 1))
                    over_k(d_bank[slot][:, :], ((lambda k: xt_hi[:, k, rows]), (lambda k: xt_lo[:, k, rows])),
                           ((lambda k: a_hi[:, k, :]), (lambda k: a_lo[:, k, :]))).then_inc(d_full[slot], 1)
                for k in range(2):
                    eng.wait_ge(d_free[k], (D_FFN + (2 * NB + 1) * h + 1 + NB + 1 - k) // 2)
                for k in range(KT):
                    slot = begin(hl_free, HL_ZT[h], 0, 0, k)
                    transposes(slot, lambda t: zg[:, t, P * k:P * (k + 1)])
                for k in range(2):
                    eng.wait_ge(hl_free[k], (HL_ZT[h] + KT) // 2)
                for k in range(KT):
                    ring_ready(R_FFN, 0, 0, 1 + KT + k)
                for t in range(NB):
                    slot = begin(d_free, D_FFN, 0, 0, (2 * NB + 1) * h + 1 + NB + t)
                    rows = slice(P * t, P * (t + 1))
                    over_k(d_bank[slot][:, :], ((lambda k: zt_hi[:, k, rows]), (lambda k: zt_lo[:, k, rows])),
                           ((lambda k: b_hi[:, k, :]), (lambda k: b_lo[:, k, :]))).then_inc(d_full[slot], 1)


PT_AT = {True: [0, 2, 4, 7], False: [0, 2, 4, 6]}
AT_AT = {True: [1, 3, 6, 9], False: [1, 3, 5, 7]}
Q_AT = [5, 8, 10, 11]


def kernel(**inputs):
    import concourse.bacc as bacc
    from concourse.bass_utils import run_bass_kernel_spmd

    a = {k: np.asarray(v) for k, v in inputs.items()}

    def tiles(w):
        k = w.shape[0] // P
        return w.reshape(k, P, w.shape[1]).transpose(1, 0, 2).reshape(P, -1)

    def rows(x):
        return x.reshape(2, NB, P, DM).transpose(0, 2, 1, 3)

    w_in_t = a["L0_attn_W_in"].T
    w_in = np.stack([np.stack([tiles(w_in_t[:, DIN * part + P * c:DIN * part + P * (c + 1)]) for part in range(2)])
                     for c in range(NC)])
    cst = np.concatenate([a["L0_attn_A_log"], a["L0_attn_conv_w"], a["L0_attn_conv_b"][:, None],
                          a["L0_attn_b_dt"][:, None], a["L0_attn_D"][:, None]], axis=1).reshape(NC, P, CST)
    w_dt = np.zeros((NC, P, P), np.float32)
    dt_t = a["L0_attn_W_dt"].T.reshape(RDT, NC, P).transpose(1, 0, 2)
    w_dt[:, 0:RDT] = dt_t
    w_dt[:, SSM:SSM + RDT] = dt_t
    ctx_t = a["ctx_4096"].reshape(TOK, DM).T.reshape(KT, P, 2, HALF).transpose(0, 2, 1, 3).reshape(2 * KT, P, HALF)
    wk_t, wv_t, wq_t = a["L0_xattn_Wk"].T, a["L0_xattn_Wv"].T, a["L0_xattn_Wq"].T
    w_kv = np.stack([np.stack([tiles(w[:, DK * g:DK * (g + 1)]) for w in (wk_t, wv_t)]) for g in range(G)])
    w_q = np.stack([np.stack([tiles(wq_t[:, DK * (HPG * g + j):DK * (HPG * g + j + 1)]) for j in range(HPG)])
                    for g in range(G)])
    w_r = np.zeros((DM, P), np.float32)
    w_r[:, 0:RDIM] = a["L0_ffn_Wq_w"].T
    keys = np.zeros((P, EXPERTS), np.float32)
    keys[0:RDIM] = a["L0_ffn_keys"].T
    arrays = {
        "x": rows(a["x"].reshape(TOK, DM)),
        "w_in": w_in,
        "cst": cst,
        "w_x": tiles(a["L0_attn_W_x"].T),
        "w_dt": w_dt,
        "w_out": a["L0_attn_W_out"].T.reshape(NC, P, DM),
        "ctx_t": ctx_t,
        "w_kv": w_kv,
        "w_q": w_q,
        "w_d": a["L0_xattn_Wd"].T.reshape(G, HPG, P, DM),
        "w_a": a["L0_ffn_A_w"].T.reshape(KT, P, DM),
        "w_b": a["L0_ffn_B_w"].T.reshape(KT, P, DM),
        "w_r": tiles(w_r),
        "keys": keys,
    }
    nc = bacc.Bacc("TRN2", target_bir_lowering=False, num_devices=1, dynamic_dma_scratch_size=1024)
    args, given = [], {}
    for name, v in arrays.items():
        given[f"in_{name}"] = np.ascontiguousarray(v)
        args.append(nc.dram_tensor(f"in_{name}", v.shape, F32, kind="ExternalInput").ap())
    args.append(nc.dram_tensor("out_rows", (2, P, NB, DM), F32, kind="ExternalOutput").ap())
    bass_decoder(nc, *args)
    r = run_bass_kernel_spmd(nc, [given], core_ids=[0])
    got = r.results[0]["out_rows"]
    return np.ascontiguousarray(got.transpose(0, 2, 1, 3)).reshape(BATCH, SEQ, DM)
```

```python
from contextlib import ExitStack

import numpy as np

import concourse.bass as bass
from concourse import mybir

F32 = mybir.dt.float32
F32R = mybir.dt.float32r
ALU = mybir.AluOpType
ACT = mybir.ActivationFunctionType
AX_X = mybir.AxisListType.X

P = 128
BATCH, SEQ, DM = 8, 128, 512
TOK = BATCH * SEQ
HALF = TOK // 2
NB = HALF // P
KT = DM // P
DIN = 1024
NC = DIN // P
NS = 16
RDT = 32
SSM = RDT + 2 * NS
TAPS = 4
G, HPG, DK = 8, 4, 128
EXPERTS, RANK, TOPK, RDIM = 64, 8, 16, 16
CH_N = 2
CHUNKS = NS // CH_N
SPREAD = NS // HPG
CST = NS + TAPS + 3
CONV0, CONVB, DTB, DSKIP = NS, NS + TAPS, NS + TAPS + 1, NS + TAPS + 2
LN_EPS, RMS_EPS = 1e-5, 1e-6
MASKED = -1e30
NEG = -3.0e38
A_LOG_MAX = 80.0

assert NC == G

HL_LN1 = 0
HL_SSM = HL_LN1 + 2 * KT
HL_KV = HL_SSM + 2
HL_LN2 = [HL_KV + 4 * G, 0]
XSTEP = 2 * NB + HPG
HL_Q = [HL_LN2[0] + KT, 0]
HL_X = [HL_Q[0] + HPG, 0]
HL_LN2[1] = HL_X[0] + XSTEP * G - HPG
HL_Q[1] = HL_LN2[1] + KT
HL_X[1] = HL_Q[1] + HPG
HL_LN3 = [HL_X[1] + XSTEP * G - HPG + 2 * KT * h for h in range(2)]
HL_ZT = [n + KT for n in HL_LN3]

S_IN = 0
S_BC = [S_IN + 4 * NC, S_IN + 4 * NC + NS]
S_X = [S_BC[1] + NS, S_BC[1] + NS + NB * G]
S_FFN = S_X[1] + NB * G

D_IN = 0
D_BC = [D_IN + 2 * NC, 0]
D_SCAN = [D_BC[0] + NS, 0]
D_BC[1] = D_SCAN[0] + NB * NC
D_X = [D_BC[1] + NS, 0]
D_SCAN[1] = D_X[0] + NB
D_SCAN_PER, D_X_PER = [NB, 2 * NB], [2 * NB, NB]
D_X[1] = D_X[0] + 2 * NB * G
D_FFN = D_X[1] + NB * G

R_WX = 0
R_IN0 = R_WX + 1
R_CTX = R_IN0 + 2
R_IN = R_CTX + 2 * KT - 2
R_KV = R_IN + 2 * NC
R_Q = [R_KV + 2 * G, 0]
R_X = [R_Q[0] + HPG, 0]
R_Q[1] = R_X[0] + HPG * G - HPG
R_X[1] = R_Q[1] + HPG
R_FFN = R_X[1] + HPG * G - HPG
R_FFN_N = 1 + 2 * KT


def use(base, per, i, k):
    n = base + k
    return n % 2, n // 2 + (per // 2) * i


class Chain:

    def __init__(self, eng, sem, per, step):
        self.eng, self.sem, self.per, self.step, self.n = eng, sem, per, step, 0

    def did(self, ins):
        ins.then_inc(self.sem, 1)
        self.n += 1

    def wait(self):
        self.eng.wait_ge(self.sem, self.per * self.step + self.n)

    def end(self):
        assert self.n == self.per, (self.n, self.per)


def steps(eng, body):
    with eng.Fori(0, NC // 2 - 1) as i:
        body(i, 0, True)
        body(i, 1, True)
    body(NC // 2 - 1, 0, True)
    body(NC // 2 - 1, 1, False)


def bass_decoder(nc, x, w_in, cst, w_x, w_dt, w_out, ctx_t, w_kv, w_q, w_d, w_a, w_b, w_r, keys, out):
    ctx = ExitStack()
    with ctx:
        def sb(name, shape, dt=F32, scope=ctx):
            return scope.enter_context(nc.sbuf_tensor(name, shape, dt))

        def sem(name):
            return ctx.enter_context(nc.semaphore(name))

        def sem2(name, n=2):
            return [sem(f"{name}{k}") for k in range(n)]

        banks = [ctx.enter_context(nc.psum_tensor(f"bank{k}", [P, HALF], F32)) for k in range(8)]
        hl_bank, s_bank, d_bank, dt_bank, y_bank = banks[0:2], banks[2:4], banks[4:6], banks[6], banks[7]

        xres = sb("xres", [P, 2 * NB, DM])
        xt_hi = sb("xt_hi", [P, KT, HALF], F32R)
        xt_lo = sb("xt_lo", [P, KT, HALF], F32R)
        ident = sb("ident", [P, P])
        ident_r = sb("ident_r", [P, P], F32R)
        mask = sb("mask", [P, P])
        mask_r = sb("mask_r", [P, P], F32R)
        raw = sb("raw", [P, 2, DM])
        ring_hi = sb("ring_hi", [P, 2, DM], F32R)
        ring_lo = sb("ring_lo", [P, 2, DM], F32R)
        cst_sb = sb("cst_sb", [P, 2, CST])
        stats = sb("stats", [P, NB, 6])
        mv = sb("mv", [P, NB, 2])
        lnv = sb("lnv", [P, NB])
        rstd = sb("rstd", [P, NB])
        eps_ln = sb("eps_ln", [P, 1])
        eps_rms = sb("eps_rms", [P, 1])
        da = sb("da", [P, 2, CH_N, HALF])
        ch = sb("ch", [P, 4, CH_N * HALF])
        xn = ch[:, 0:2, :].rearrange("p a (b d) -> p (a b) d", d=DM)
        stk = sb("stk", [P, 2, HALF], F32R)

        u_dram = nc.dram_tensor("u_spill", [2, NC, P, HALF], F32, kind="Internal").ap()
        sg_dram = nc.dram_tensor("sg_spill", [2, NC, P, HALF], F32, kind="Internal").ap()
        kv_dram = nc.dram_tensor("kv_spill", [G, 4, P, 2, HALF], F32, kind="Internal").ap()

        def overlaid(name, lo, shape, scope):
            with ExitStack() as landing:
                raw_part = sb(name, shape, F32, landing)
            return raw_part, sb(lo, shape, F32R, scope)

        def scan_buffers(scope):
            wo, wo_lo = overlaid("wo", "wo_lo", [P, DM], scope)
            return dict(
                wo=wo, wo_lo=wo_lo,
                bc=sb("bc", [P, 2 * NS, HALF], F32, scope),
                u=sb("u_in", [P, 2, HALF], F32, scope),
                sg=sb("sg_in", [P, HALF], F32, scope),
                wdt=sb("wdt", [P, P], F32, scope),
                wdt_hi=sb("wdt_hi", [P, P], F32R, scope),
                wdt_lo=sb("wdt_lo", [P, P], F32R, scope),
                wo_hi=sb("wo_hi", [P, DM], F32R, scope),
                ea=sb("ea", [P, 2, NS], F32, scope),
                na=sb("na", [P, 2, NS], F32, scope),
                dt=sb("dt", [P, 2, HALF], F32, scope),
                dtu=sb("dtu", [P, HALF], F32, scope),
                sp=sb("sp", [P, HALF], F32, scope),
                rl=sb("rl", [P, HALF], F32, scope),
                y=sb("y", [P, HALF], F32, scope),
                y_hi=sb("y_hi", [P, HALF], F32R, scope),
                y_lo=sb("y_lo", [P, HALF], F32R, scope),
            )

        with ExitStack() as sc:
            xt1_hi = sb("xt1_hi", [P, KT, HALF], F32R, sc)
            xt1_lo = sb("xt1_lo", [P, KT, HALF], F32R, sc)
            wx_hi = sb("wx_hi", [P, NC * SSM], F32R, sc)
            wx_lo = sb("wx_lo", [P, NC * SSM], F32R, sc)
            wx_step = sb("wx_step", [P, 2, 2, SSM], F32R, sc)
            xpad = sb("xpad", [P, 2, NB, TAPS - 1 + SEQ], F32, sc)
            conv = sb("conv", [P, 2, HALF], F32, sc)
            u_out = sb("u_out", [P, 2, 2, HALF], F32, sc)
            sg_out = sb("sg_out", [P, 2, 2, HALF], F32, sc)
            u_hi = sb("u_hi", [P, 2, HALF], F32R, sc)
            u_lo = sb("u_lo", [P, 2, HALF], F32R, sc)
            ssm = sb("ssm", [P, 2 * NB, SSM], F32, sc)
            ssm_sq = sb("ssm_sq", [P, 2 * NB, SSM], F32, sc)
            ssm_n = sb("ssm_n", [P, 2 * NB, 2, SSM], F32, sc)
            ssm_ss = sb("ssm_ss", [P, 3, 2 * NB], F32, sc)
            ssm_ln = sb("ssm_ln", [P, 3, 2 * NB], F32, sc)
            ssm_rs = sb("ssm_rs", [P, 3, 2 * NB], F32, sc)
            stk_t = sb("stk_t", [P, HALF], F32R, sc)

        sc_scan = ExitStack()
        B = scan_buffers(sc_scan)
        with ExitStack() as sc:
            ctx_hi = sb("ctx_hi", [P, KT, TOK], F32R, sc)
            ctx_lo = sb("ctx_lo", [P, KT, TOK], F32R, sc)
            stg_hi = sb("stg_hi", [P, 2, HALF], F32R, sc)
            stg_lo = sb("stg_lo", [P, 2, HALF], F32R, sc)
            sel_c = sb("sel_c", [P, 2 * NS], F32, sc)
            sel = sb("sel", [P, 2 * NS, P], F32R, sc)
        with ExitStack() as sc:
            q_hi = sb("q_hi", [P, HPG, HALF], F32R, sc)
            q_lo = sb("q_lo", [P, HPG, HALF], F32R, sc)
            kv = sb("kv", [P, 2, 2, HALF], F32R, sc)
            pr = sb("pr", [P, 2, HPG, P], F32, sc)
            pt_hi = sb("pt_hi", [P, HALF], F32R, sc)
            pt_lo = sb("pt_lo", [P, HALF], F32R, sc)
            at_hi = sb("at_hi", [P, 2, HALF], F32R, sc)
            at_lo = sb("at_lo", [P, 2, HALF], F32R, sc)
            wd_hi = sb("wd_hi", [P, HPG, DM], F32R, sc)
            wd, wd_lo = overlaid("wd", "wd_lo", [P, HPG, DM], sc)
            mx = sb("mx", [P, 2, HPG], F32, sc)
            nmx = sb("nmx", [P, 2, HPG], F32, sc)
            psum_row = sb("psum_row", [P, 2, HPG], F32, sc)
            rcp = sb("rcp", [P, 2, HPG], F32, sc)
        sc_scan.close()
        with ExitStack() as sc:
            a_hi = sb("a_hi", [P, KT, DM], F32R, sc)
            a_lo = sb("a_lo", [P, KT, DM], F32R, sc)
            b_hi = sb("b_hi", [P, KT, DM], F32R, sc)
            b_lo = sb("b_lo", [P, KT, DM], F32R, sc)
            r_hi = sb("r_hi", [P, DM], F32R, sc)
            r_lo = sb("r_lo", [P, DM], F32R, sc)
            keys_sb = sb("keys_sb", [P, EXPERTS], F32, sc)
            qr = sb("qr", [P, HALF], F32, sc)
            sco = sb("sco", [P, NB, EXPERTS], F32, sc)
            sco1 = sb("sco1", [P, NB, EXPERTS], F32, sc)
            sco2 = sb("sco2", [P, NB, EXPERTS], F32, sc)
            top = sb("top", [P, NB, 2, 8], F32, sc)
            ntop = sb("ntop", [P, NB], F32, sc)
            gsum = sb("gsum", [P, NB], F32, sc)
            grcp = sb("grcp", [P, NB], F32, sc)
            picked = sb("picked", [P, NB, EXPERTS], F32, sc)
            ge = sb("ge", [P, NB, EXPERTS], F32, sc)
            zg = sb("zg", [P, NB, DM], F32, sc)
            zt_hi = sb("zt_hi", [P, KT, HALF], F32R, sc)
            zt_lo = sb("zt_lo", [P, KT, HALF], F32R, sc)
            res = sb("res", [P, 2 * NB, DM], F32, sc)

        x_in, const_ok, masks_ok = sem2("x_in"), sem("const_ok"), sem("masks_ok")
        hl_full, hl_hi, hl_free = sem2("hl_full"), sem2("hl_hi"), sem2("hl_free")
        s_full, s_free = sem2("s_full"), sem2("s_free")
        d_full, d_free = sem2("d_full"), sem2("d_free")
        raw_in, w_hi_ok, w_ok = sem2("raw_in"), sem2("w_hi_ok"), sem2("w_ok")
        ln_mv, ln_stat, ln_rstd, ln_xn = sem("ln_mv"), sem("ln_stat"), sem("ln_rstd"), sem("ln_xn")
        cst_in = sem2("cst_in")
        pad_ok, conv_ch, conv_ok, silu_ok = sem("pad_ok"), sem("conv_ch"), sem("conv_ok"), sem("silu_ok")
        wx_ok = sem("wx_ok")
        uhi_ok, ulo_ok, gate_ok = sem("uhi_ok"), sem("ulo_ok"), sem("gate_ok")
        spill = sem2("spill")
        ssm_ch, ssm_rs_ok, stk_cp = sem("ssm_ch"), sem("ssm_rs_ok"), sem("stk_cp")
        stg_out = sem2("stg_out")
        sel_ok, zero_ok = sem("sel_ok"), sem("zero_ok")
        scan_in, sg_in, ws_in, wo_in = sem2("scan_in"), sem("sg_in"), sem("ws_in"), sem("wo_in")
        wd_in, wd_hi_ok, wd_ok = sem("wd_in"), sem("wd_hi_ok"), sem("wd_ok")
        wdt_hi_ok, wdt_ok, wo_hi_ok, wo_ok = sem("wdt_hi_ok"), sem("wdt_ok"), sem("wo_hi_ok"), sem("wo_ok")
        dt_full, dt_abs, dt_free, dt_exp, dt_ln = (sem("dt_full"), sem("dt_abs"), sem("dt_free"), sem("dt_exp"),
                                                   sem("dt_ln"))
        al_ok, dt_err, dt_rest = sem("al_ok"), sem("dt_err"), sem("dt_rest")
        ea_ok, na_ok, dt_ok, dtu_ok = sem("ea_ok"), sem("na_ok"), sem("dt_ok"), sem("dtu_ok")
        da_full, scan_done = sem2("da_full"), sem2("scan_done")
        ch_full, ch_mul, ch_free = sem2("ch_full", 4), sem2("ch_mul", 4), sem2("ch_free", 4)
        ch_pair = sem2("ch_pair", 4)
        y_full, y_free, y_ok, yhi_ok, ylo_ok = (sem("y_full"), sem("y_free"), sem("y_ok"), sem("yhi_ok"),
                                                sem("ylo_ok"))
        k_in, v_in, mx_ch, mx_ok, sum_ok, rcp_ok, pn_ok = (sem("k_in"), sem("v_in"), sem("mx_ch"), sem("mx_ok"), sem("sum_ok"),
                                                      sem("rcp_ok"), sem("pn_ok"))
        keys_in, qr_ok, ffn_ch, ge_ok, gate_f, zg_ok, out_ok, stored = (
            sem("keys_in"), sem("qr_ok"), sem("ffn_ch"), sem("ge_ok"), sem("gate_f"), sem("zg_ok"),
            sem("out_ok"), sem("stored"))
        block = ctx.enter_context(nc.Block())

        def kv_load(eng, h, g, k):
            eng.dma_start(kv[:, k, :, :].bitcast(F32), kv_dram[g, 2 * k + h]).then_inc((k_in, v_in)[k], 16)

        def wd_load(eng, g):
            eng.dma_start(wd[:, :, :], w_d[g]).then_inc(wd_in, 16)

        @block.sync
        def _(eng):
            def ring_load(base, per, i, k, src):
                slot, n = use(base, per, i, k)
                eng.wait_ge(w_ok[slot], n)
                eng.dma_start(raw[:, slot, :], src).then_inc(raw_in[slot], 16)

            eng.dma_start(xres[:, 0:NB, :], x[0]).then_inc(x_in[0], 16)
            ring_load(R_WX, 0, 0, 0, w_x)
            ring_load(R_IN0, 2, 0, 0, w_in[0, 0])
            eng.dma_start(xres[:, NB:2 * NB, :], x[1]).then_inc(x_in[1], 16)
            eng.dma_start(cst_sb[:, 0, :], cst[0]).then_inc(cst_in[0], 16)
            ring_load(R_IN0, 2, 0, 1, w_in[0, 1])
            for k in range(2 * KT):
                ring_load(R_CTX, 0, 0, k, ctx_t[k])

            def in_step(i, p, nxt):
                c = 2 * i + p
                if nxt:
                    if p == 0:
                        eng.wait_ge(conv_ok, 4 * i)
                    else:
                        eng.wait_ge(conv_ok, 4 * i + 2)
                    eng.dma_start(cst_sb[:, 1 - p, :], cst[c + 1]).then_inc(cst_in[1 - p], 16)
                    for k in range(2):
                        ring_load(R_IN + 2 * p, 4, i, 2 + k, w_in[c + 1, k])
                eng.wait_ge(gate_ok, 2 * c + 2)
                for h in range(2):
                    eng.dma_start(sg_dram[h, c], sg_out[:, p, h, :]).then_inc(spill[p], 16)
                eng.wait_ge(silu_ok, 2 * c + 2)
                for h in range(2):
                    eng.dma_start(u_dram[h, c], u_out[:, p, h, :]).then_inc(spill[p], 16)
            steps(eng, in_step)

            for k in range(2):
                ring_load(R_KV, 2, 0, k, w_kv[0, k])
            for p in range(2):
                eng.wait_ge(spill[p], 4 * 16 * (NC // 2))

            def scan_load(h, i, p):
                c, s = 2 * i + p, NC * h + 2 * i + p
                if h or not isinstance(i, int) or s >= 2:
                    eng.wait_ge(y_free, s - 1)
                eng.dma_start(B["u"][:, p, :], u_dram[h, c]).then_inc(scan_in[p], 16)
                eng.dma_start(cst_sb[:, p, :], cst[c]).then_inc(scan_in[p], 16)
                eng.wait_ge(wdt_ok, s)
                eng.dma_start(B["wdt"][:, :], w_dt[c]).then_inc(ws_in, 16)

            def scan_step(h, i, p, nxt):
                c, s = 2 * i + p, NC * h + 2 * i + p
                if nxt:
                    if p == 0:
                        scan_load(h, i, 1)
                    else:
                        scan_load(h, i + 1, 0)
                slot, n = use(D_SCAN[h] + D_SCAN_PER[h] * p, 2 * D_SCAN_PER[h], i, NB - 1 - D_SCAN_PER[h])
                eng.wait_ge(d_full[slot], n + 1)
                eng.dma_start(B["sg"][:, :], sg_dram[h, c]).then_inc(sg_in, 16)
                eng.dma_start(B["wo"][:, :], w_out[c]).then_inc(wo_in, 16)

            def kv_step(i, p, nxt):
                g = 2 * i + p
                scan_step(0, i, p, nxt)
                if nxt:
                    for k in range(2):
                        ring_load(R_KV + 2 * p, 4, i, 2 + k, w_kv[g + 1, k])
                for k in range(2, 6 if nxt else 4):
                    stage_out(i, p, k)

            def stage_out(i, p, k):
                g = 2 * i + p + k // 4
                slot, n = use(HL_KV + 4 * p, 8, i, k)
                eng.wait_ge(hl_free[slot], n + 1)
                eng.dma_start(kv_dram[g, k % 4, :, 0, :], stg_hi[:, slot, :].bitcast(F32)).then_inc(stg_out[slot], 16)
                eng.dma_start(kv_dram[g, k % 4, :, 1, :], stg_lo[:, slot, :].bitcast(F32)).then_inc(stg_out[slot], 16)

            scan_load(0, 0, 0)
            for k in range(2):
                stage_out(0, 0, k)
            steps(eng, kv_step)
            scan_load(1, 0, 0)
            for p in range(2):
                eng.wait_ge(stg_out[p], 2 * 16 * (4 * G // 2))

            def x_step(h, i, p, nxt, scan=None):
                g = 2 * i + p

                def q_load(j):
                    if nxt:
                        ring_load(R_X[h] + HPG * p, 2 * HPG, i, j, w_q[g + 1, j])

                q_load(0)
                q_load(1)
                if scan:
                    scan(i, p, nxt)
                q_load(2)
                if nxt:
                    slot, n = use(S_X[h] + NB * p, 2 * NB, i, NB - 1)
                    eng.wait_ge(s_full[slot], n + 1)
                    kv_load(eng, h, g + 1, 0)
                q_load(3)

            for h in range(2):
                for j in range(HPG):
                    ring_load(R_Q[h], 0, 0, j, w_q[0, j])
                for k in range(2):
                    eng.wait_ge(hl_full[k], HL_LN2[h] // 2)
                    eng.wait_ge(d_full[k], D_X[h] // 2)
                kv_load(eng, h, 0, 0)
                kv_load(eng, h, 0, 1)
                wd_load(eng, 0)
                if h == 0:
                    steps(eng, lambda i, p, nxt: x_step(0, i, p, nxt, lambda *at: scan_step(1, *at)))
                else:
                    steps(eng, lambda i, p, nxt: x_step(1, i, p, nxt))

            ring_load(R_FFN, 0, 0, 0, w_r)
            for k in range(KT):
                ring_load(R_FFN, 0, 0, 1 + k, w_a[k])
            for k in range(KT):
                ring_load(R_FFN, 0, 0, 1 + KT + k, w_b[k])
            for p in range(2):
                eng.wait_ge(hl_full[p], HL_LN3[0] // 2)
            eng.dma_start(keys_sb[:, :], keys).then_inc(keys_in, 16)
            for h in range(2):
                eng.wait_ge(out_ok, NB * (h + 1))
                eng.dma_start(out[h], res[:, NB * h:NB * (h + 1), :]).then_inc(stored, 16)
            eng.wait_ge(stored, 32)

        @block.gpsimd
        def _(eng):
            eng.memset(ident[:, :], 0.0).then_inc(const_ok, 1)
            eng.memset(mask[:, :], 0.0).then_inc(const_ok, 1)
            eng.memset(eps_ln[:, :], LN_EPS).then_inc(const_ok, 1)
            eng.memset(eps_rms[:, :], RMS_EPS).then_inc(const_ok, 1)
            eng.wait_ge(const_ok, 4)
            eng.affine_select(out=ident[:, :], in_=ident[:, :], compare_op=ALU.not_equal, fill=1.0, base=0,
                              pattern=[[-1, P]], channel_multiplier=1).then_inc(const_ok, 1)
            eng.affine_select(out=mask[:, :], in_=mask[:, :], compare_op=ALU.is_ge, fill=MASKED, base=0,
                              pattern=[[-1, P]], channel_multiplier=1).then_inc(const_ok, 1)

            def ring_lo_part(base, per, i, k, lo, hi):
                slot, n = use(base, per, i, k)
                eng.wait_ge(w_hi_ok[slot], n + 1)
                nc.gpsimd.tensor_tensor(lo, raw[:, slot, :], hi, ALU.subtract).then_inc(w_ok[slot], 1)

            ring_lo_part(R_WX, 0, 0, 0, wx_lo[:, :], wx_hi[:, :].bitcast(F32))
            for k in range(2):
                ring_lo_part(R_IN0, 2, 0, k, ring_lo[:, k, :], ring_hi[:, k, :].bitcast(F32))
            for k in range(2 * KT):
                at = (slice(None), k // 2, slice(HALF * (k % 2), HALF * (k % 2 + 1)))
                ring_lo_part(R_CTX, 0, 0, k, ctx_lo[at], ctx_hi[at].bitcast(F32))

            def in_step(i, p, nxt):
                if nxt:
                    for k in range(2):
                        ring_lo_part(R_IN + 2 * p, 4, i, 2 + k, ring_lo[:, k, :], ring_hi[:, k, :].bitcast(F32))
            steps(eng, in_step)
            for k in range(2):
                ring_lo_part(R_KV, 2, 0, k, ring_lo[:, k, :], ring_hi[:, k, :].bitcast(F32))

            def kv_step(i, p, nxt):
                def split(k):
                    if nxt:
                        ring_lo_part(R_KV + 2 * p, 4, i, 2 + k, ring_lo[:, k, :], ring_hi[:, k, :].bitcast(F32))

                scan_chunk(0, i, p, nxt, 4)
                scan_chunk(0, i, p, nxt, 5)
                if nxt:
                    scan_prep_w(0, i + p, 1 - p)
                split(0)
                scan_chunk(0, i, p, nxt, 6)
                scan_chunk(0, i, p, nxt, 7)
                if nxt:
                    scan_prep_u(0, i + p, 1 - p)
                scan_chunk(0, i, p, nxt, 8)
                split(1)
                scan_wo_lo(0, i, p)
                scan_chunk(0, i, p, nxt, 9)
                scan_chunk(0, i, p, nxt, 10)
                scan_chunk(0, i, p, nxt, 11)

            def scan_prep_w(h, i, p):
                s = NC * h + 2 * i + p
                eng.wait_ge(wdt_hi_ok, s + 1)
                nc.gpsimd.tensor_tensor(B["wdt_lo"][:, :], B["wdt"][:, :], B["wdt_hi"][:, :].bitcast(F32),
                                        ALU.subtract).then_inc(wdt_ok, 1)

            def scan_prep_u(h, i, p):
                s = NC * h + 2 * i + p
                eng.wait_ge(dt_ok, s + 1)
                eng.wait_ge(ch_full[3], 2 * s)
                nc.gpsimd.tensor_tensor(B["dtu"][:, :], B["dt"][:, p, :], B["u"][:, p, :],
                                        ALU.mult).then_inc(dtu_ok, 1)

            def scan_chunk(h, i, p, nxt, j):
                s, slot = NC * h + 2 * i + p, j % 4
                if j >= CHUNKS and not nxt:
                    return
                if j % CHUNKS == 0:
                    eng.wait_ge(dtu_ok, s + j // CHUNKS + 1)
                eng.wait_ge(ch_free[slot], 2 * s + j // 4)
                n = CH_N * (j % CHUNKS)
                nc.gpsimd.tensor_tensor(
                    ch[:, slot, :].rearrange("p (n t) -> p n t", n=CH_N),
                    B["dtu"][:, None, :].broadcast_to([P, CH_N, HALF]),
                    B["bc"][:, n:n + CH_N, :], ALU.mult).then_inc(ch_full[slot], 1)

            def scan_wo_lo(h, i, p):
                eng.wait_ge(wo_hi_ok, NC * h + 2 * i + p + 1)
                nc.gpsimd.tensor_tensor(B["wo_lo"][:, :], B["wo"][:, :],
                                        B["wo_hi"][:, :].bitcast(F32), ALU.subtract).then_inc(wo_ok, 1)

            def scan_start(h):
                scan_prep_u(h, 0, 0)
                for k in range(2):
                    eng.wait_ge(s_free[k], (S_BC[h] + NS // 2) // 2)
                    eng.wait_ge(d_free[k], (D_BC[h] + NS // 2) // 2)
                for j in range(4):
                    scan_chunk(h, 0, 0, True, j)

            def x_step(h, i, p, nxt, scan=False):
                s = G * h + 2 * i + p

                def chunk(j):
                    if scan:
                        scan_chunk(1, i, p, nxt, j)

                def split_q(j):
                    if nxt:
                        ring_lo_part(R_X[h] + HPG * p, 2 * HPG, i, j, ring_lo[:, j % 2, :],
                                     ring_hi[:, j % 2, :].bitcast(F32))

                def split_d(j):
                    eng.wait_ge(wd_hi_ok, HPG * s + j + 1)
                    nc.gpsimd.tensor_tensor(wd_lo[:, j, :], wd[:, j, :], wd_hi[:, j, :].bitcast(F32),
                                            ALU.subtract).then_inc(wd_ok, 1)

                normalise(h, i, p, 2)
                split_q(0)
                if scan and nxt:
                    scan_prep_w(1, i + p, 1 - p)
                chunk(4)
                split_d(0)
                split_d(1)
                split_d(2)
                split_d(3)
                chunk(5)
                normalise(h, i, p, 3)
                split_q(1)
                split_q(2)
                chunk(6)
                chunk(7)
                split_q(3)
                if scan and nxt:
                    scan_prep_u(1, i + p, 1 - p)
                chunk(8)
                if scan:
                    scan_wo_lo(1, i, p)
                chunk(9)
                chunk(10)
                chunk(11)
                if nxt:
                    normalise(h, i, p, NB)
                    normalise(h, i, p, NB + 1)

            def normalise(h, i, p, b):
                eng.wait_ge(rcp_ok, NB * (G * h + 2 * i + p) + b + 1)
                nc.gpsimd.tensor_tensor(pr[:, b % 2, :, :], pr[:, b % 2, :, :],
                                        rcp[:, b % 2, :, None].broadcast_to([P, HPG, P]),
                                        ALU.mult).then_inc(pn_ok, 1)

            scan_prep_w(0, 0, 0)
            scan_start(0)
            steps(eng, kv_step)
            for h in range(2):
                for j in range(HPG):
                    ring_lo_part(R_Q[h], 0, 0, j, ring_lo[:, j % 2, :], ring_hi[:, j % 2, :].bitcast(F32))
                    if h == 0 and j == 0:
                        scan_prep_w(1, 0, 0)
                if h == 0:
                    scan_start(1)
                for b in range(2):
                    normalise(h, 0, 0, b)
                steps(eng, lambda i, p, nxt: x_step(h, i, p, nxt, h == 0))
            ring_lo_part(R_FFN, 0, 0, 0, r_lo[:, :], r_hi[:, :].bitcast(F32))
            for k in range(KT):
                ring_lo_part(R_FFN, 0, 0, 1 + k, a_lo[:, k, :], a_hi[:, k, :].bitcast(F32))
            for k in range(KT):
                ring_lo_part(R_FFN, 0, 0, 1 + KT + k, b_lo[:, k, :], b_hi[:, k, :].bitcast(F32))

        @block.scalar
        def _(eng):
            act = nc.scalar.activation

            def ring_hi_part(base, per, i, k, hi):
                slot, n = use(base, per, i, k)
                eng.wait_ge(raw_in[slot], 16 * n + 16)
                act(hi, raw[:, slot, :], ACT.Copy).then_inc(w_hi_ok[slot], 1)

            def hl_part(base, per, i, k, hi):
                slot, n = use(base, per, i, k)
                eng.wait_ge(hl_full[slot], n + 1)
                act(hi, hl_bank[slot][:, :], ACT.Copy).then_inc(hl_hi[slot], 1)

            def load_table(name):
                nc.scalar.preload_act_table_set(name)

            def ln_rstd_part(l):
                eng.wait_ge(ln_stat, l + 1)
                act(lnv[:, :], mv[:, :, 1], ACT.Ln, bias=eps_ln[:, :]).then_inc(ln_rstd, 1)
                eng.wait_ge(ln_rstd, 2 * l + 1)
                act(rstd[:, :], lnv[:, :], ACT.Exp, scale=-0.5).then_inc(ln_rstd, 1)

            eng.wait_ge(const_ok, 6)
            load_table("natural_log_exp_and_others")
            act(ident_r[:, :], ident[:, :], ACT.Copy).then_inc(masks_ok, 1)
            act(mask_r[:, :], mask[:, :], ACT.Copy).then_inc(masks_ok, 1)
            ring_hi_part(R_WX, 0, 0, 0, wx_hi[:, :])
            for k in range(2):
                ring_hi_part(R_IN0, 2, 0, k, ring_hi[:, k, :])
            for h in range(2):
                ln_rstd_part(h)
                for k in range(KT):
                    hl_part(HL_LN1, 0, 0, KT * h + k, (xt_hi, xt1_hi)[h][:, k, :])
                    n = KT * h + k
                    ring_hi_part(R_CTX, 0, 0, n, ctx_hi[:, n // 2, HALF * (n % 2):HALF * (n % 2 + 1)])
            eng.wait_ge(zero_ok, 1)

            def pad_rows(i, p, h, k):
                slot, n = use(S_IN + 4 * p, 8, i, k)
                eng.wait_ge(s_full[slot], n + 1)
                eng.wait_ge(conv_ok, 2 * (2 * i + p + k // 4))
                act(xpad[:, h, :, TAPS - 1:], s_bank[slot][:, :].rearrange("p (b t) -> p b t", b=NB),
                    ACT.Copy).then_inc(s_free[slot], 1)

            for h in range(2):
                pad_rows(0, 0, h, h)

            def in_step(i, p, nxt):
                c = 2 * i + p
                if nxt:
                    ring_hi_part(R_IN + 2 * p, 4, i, 2, ring_hi[:, 0, :])
                for h in range(2):
                    slot, n = use(S_IN + 4 * p, 8, i, 2 + h)
                    eng.wait_ge(s_full[slot], n + 1)
                    if h == 0:
                        eng.wait_ge(spill[p], 64 * i)
                    act(sg_out[:, p, h, :], s_bank[slot][:, :], ACT.Silu).then_inc(gate_ok, 1)
                    eng.wait_ge(gate_ok, 2 * c + h + 1)
                    eng.sem_inc(s_free[slot], 1)
                if nxt:
                    ring_hi_part(R_IN + 2 * p, 4, i, 3, ring_hi[:, 1, :])
                for h in range(2):
                    eng.wait_ge(conv_ok, 2 * c + h + 1)
                    act(u_out[:, p, h, :], conv[:, h, :], ACT.Silu).then_inc(silu_ok, 1)
                    eng.wait_ge(silu_ok, 2 * c + h + 1)
                    eng.wait_ge(d_full[(D_IN + h) % 2], D_IN // 2 + c)
                    act(u_hi[:, h, :], u_out[:, p, h, :], ACT.Copy).then_inc(uhi_ok, 1)
                if nxt:
                    for h in range(2):
                        pad_rows(i, p, h, 4 + h)
            steps(eng, in_step)
            for k in range(2):
                ring_hi_part(R_KV, 2, 0, k, ring_hi[:, k, :])

            load_table("natural_log_exp_and_others")
            eng.wait_ge(ssm_ch, 4)
            act(ssm_ln[:, 0, :], ssm_ss[:, 0, :], ACT.Ln, bias=eps_rms[:, :], scale=1.0 / RDT).then_inc(ssm_rs_ok, 1)
            act(ssm_ln[:, 1:3, :], ssm_ss[:, 1:3, :], ACT.Ln, bias=eps_rms[:, :],
                scale=1.0 / NS).then_inc(ssm_rs_ok, 1)
            eng.wait_ge(ssm_rs_ok, 2)
            act(ssm_rs[:, :, :], ssm_ln[:, :, :], ACT.Exp, scale=-0.5).then_inc(ssm_rs_ok, 1)
            for h in range(2):
                slot, n = use(HL_SSM, 0, 0, h)
                eng.wait_ge(hl_full[slot], n + 1)
                act(stk[0:SSM, h, :], hl_bank[slot][0:SSM, :], ACT.Copy).then_inc(stk_cp, 1)
                if h:
                    eng.wait_ge(hl_free[use(HL_SSM, 0, 0, 0)[0]], use(HL_SSM, 0, 0, 0)[1] + 1)
                act(stk_t[SSM:P, :], hl_bank[slot][SSM:P, :], ACT.Copy).then_inc(hl_hi[slot], 1)
            def stage(i, p, k):
                slot, n = use(HL_KV + 4 * p, 8, i, k)
                eng.wait_ge(stg_out[slot], 32 * (n - HL_KV // 2))
                hl_part(HL_KV + 4 * p, 8, i, k, stg_hi[:, slot, :])

            def kv_step(i, p, nxt):
                def split(k):
                    if nxt:
                        ring_hi_part(R_KV + 2 * p, 4, i, 2 + k, ring_hi[:, k, :])

                scan_chunk(0, i, p, nxt, 4)
                if nxt:
                    scan_prep_w(0, i + p, 1 - p)
                split(0)
                scan_chunk(0, i, p, nxt, 5)
                stage(i, p, 2)
                if nxt:
                    scan_prep(0, i + p, 1 - p)
                scan_chunk(0, i, p, nxt, 6)
                if nxt:
                    scan_prep_ln(0, i + p, 1 - p)
                stage(i, p, 3)
                split(1)
                scan_chunk(0, i, p, nxt, 7)
                scan_wo_hi(0, i, p)
                scan_chunk(0, i, p, nxt, 8)
                if nxt:
                    stage(i, p, 4)
                scan_chunk(0, i, p, nxt, 9)
                scan_chunk(0, i, p, nxt, 10)
                scan_y_hi(0, i, p)
                if nxt:
                    stage(i, p, 5)
                scan_chunk(0, i, p, nxt, 11)

            def scan_prep_w(h, i, p):
                s = NC * h + 2 * i + p
                eng.wait_ge(ws_in, 16 * s + 16)
                eng.wait_ge(dt_full, s)
                act(B["wdt_hi"][:, :], B["wdt"][:, :], ACT.Copy).then_inc(wdt_hi_ok, 1)

            def scan_prep(h, i, p):
                s, n = NC * h + 2 * i + p, (NC // 2) * h + i
                eng.wait_ge(scan_in[p], 32 * n + 32)
                eng.wait_ge(al_ok, s + 1)
                act(B["ea"][:, p, :], B["ea"][:, p, :], ACT.Exp).then_inc(ea_ok, 1)
                eng.wait_ge(dt_full, s + 1)
                eng.wait_ge(dt_ok, s)
                act(B["sp"][:, :], dt_bank[:, :], ACT.Abs, bias=cst_sb[:, p, DTB:DTB + 1]).then_inc(dt_abs, 1)
                eng.wait_ge(dt_abs, s + 1)
                act(B["sp"][:, :], B["sp"][:, :], ACT.Exp, scale=-1.0).then_inc(dt_exp, 1)
                eng.wait_ge(dt_exp, 2 * s + 1)
                act(B["dt"][:, p, :], B["sp"][:, :], ACT.Identity, bias=1.0).then_inc(dt_exp, 1)

            def scan_prep_ln(h, i, p):
                s = NC * h + 2 * i + p
                eng.wait_ge(dt_err, s + 1)
                act(B["dt"][:, p, :], B["dt"][:, p, :], ACT.Ln).then_inc(dt_ln, 1)

            def scan_chunk(h, i, p, nxt, j):
                s, slot, q = NC * h + 2 * i + p, j % 2, (p + j // CHUNKS) % 2
                if j >= CHUNKS and not nxt:
                    return
                if j % CHUNKS == 0:
                    eng.wait_ge(dt_ok, s + j // CHUNKS + 1)
                    eng.wait_ge(na_ok, s + j // CHUNKS + 1)
                eng.wait_ge(scan_done[slot], 4 * s + j // 2)
                for m in range(CH_N):
                    n = CH_N * (j % CHUNKS) + m
                    last = act(da[:, slot, m, :].rearrange("p (b t) -> p b t", b=NB)[:, :, 1:],
                               B["dt"][:, q, :].rearrange("p (b t) -> p b t", b=NB)[:, :, 1:], ACT.Exp,
                               scale=B["na"][:, q, n:n + 1])
                last.then_inc(da_full[slot], 1)

            def scan_wo_hi(h, i, p):
                eng.wait_ge(wo_in, 16 * (NC * h + 2 * i + p) + 16)
                act(B["wo_hi"][:, :], B["wo"][:, :], ACT.Copy).then_inc(wo_hi_ok, 1)

            def scan_y_hi(h, i, p):
                eng.wait_ge(y_ok, NC * h + 2 * i + p + 1)
                act(B["y_hi"][:, :], B["y"][:, :], ACT.Copy).then_inc(yhi_ok, 1)

            def spread(h, first, last):
                for k in range(first, last):
                    slot, n = use(S_BC[h], 0, 0, k)
                    eng.wait_ge(s_full[slot], n + 1)
                    act(B["bc"][:, 2 * k, :], s_bank[slot][:, :], ACT.Copy).then_inc(s_free[slot], 1)

            def scan_start(h):
                for j in range(4):
                    scan_chunk(h, 0, 0, True, j)

            def probs(h, i, p, b):
                slot, n = use(S_X[h] + NB * p, 2 * NB, i, b)
                eng.wait_ge(mx_ok, NB * (G * h + 2 * i + p) + b + 1)
                for j in range(HPG):
                    last = act(pr[:, b % 2, j, :], s_bank[slot][:, P * j:P * (j + 1)], ACT.Exp,
                               bias=nmx[:, b % 2, j:j + 1], scale=DK ** -0.5,
                               accum_out=psum_row[:, b % 2, j:j + 1])
                last.then_inc(sum_ok, 1)

            def x_step(h, i, p, nxt, scan=False):
                s = G * h + 2 * i + p

                def chunk(j):
                    if scan:
                        scan_chunk(1, i, p, nxt, j)

                def hl(k, hi):
                    hl_part(HL_X[h] + XSTEP * p, 2 * XSTEP, i, k, hi)

                def turned(b):
                    hl(PT_AT[nxt][b], pt_hi[:, :])

                def attended(b):
                    sl, m = use(D_X[h] + D_X_PER[h] * p, 2 * D_X_PER[h], i, b - 2 if b >= 2 else b + 2 - D_X_PER[h])
                    eng.wait_ge(d_full[sl], m + 1)
                    hl(AT_AT[nxt][b], at_hi[:, b % 2, :])

                def next_q(j):
                    if nxt:
                        hl(Q_AT[j], q_hi[:, j, :])

                def split_q(j):
                    if nxt:
                        ring_hi_part(R_X[h] + HPG * p, 2 * HPG, i, j, ring_hi[:, j % 2, :])

                def split_d(j):
                    eng.wait_ge(wd_in, 16 * s + 16)
                    act(wd_hi[:, j, :], wd[:, j, :], ACT.Copy).then_inc(wd_hi_ok, 1)

                turned(0)
                probs(h, i, p, 2)
                attended(0)
                split_q(0)
                turned(1)
                if scan and nxt:
                    scan_prep_w(1, i + p, 1 - p)
                split_d(0)
                chunk(4)
                attended(1)
                split_d(1)
                chunk(5)
                turned(2)
                split_d(2)
                split_d(3)
                probs(h, i, p, 3)
                split_q(1)
                if scan and nxt:
                    scan_prep(1, i + p, 1 - p)
                next_q(0)
                split_q(2)
                chunk(6)
                if scan and nxt:
                    scan_prep_ln(1, i + p, 1 - p)
                next_q(1)
                split_q(3)
                attended(2)
                chunk(7)
                if scan:
                    scan_wo_hi(1, i, p)
                chunk(8)
                turned(3)
                next_q(2)
                chunk(9)
                attended(3)
                if nxt:
                    kv_load(eng, h, 2 * i + p + 1, 1)
                chunk(10)
                next_q(3)
                if scan:
                    scan_y_hi(1, i, p)
                if nxt:
                    probs(h, i, p, NB)
                    chunk(11)
                    probs(h, i, p, NB + 1)
                    slot, n = use(D_X[h] + D_X_PER[h] * p, 2 * D_X_PER[h], i, NB - 1)
                    eng.wait_ge(d_full[slot], n + 1)
                    wd_load(eng, 2 * i + p + 1)

            scan_prep_w(0, 0, 0)
            scan_prep(0, 0, 0)
            scan_prep_ln(0, 0, 0)
            spread(0, 0, NS)
            scan_start(0)
            for k in range(2):
                stage(0, 0, k)
            steps(eng, kv_step)
            for h in range(2):
                ln_rstd_part(2 + h)
                for k in range(KT):
                    hl_part(HL_LN2[h], 0, 0, k, xt_hi[:, k, :])
                if h == 0:
                    for k in range(2):
                        eng.wait_ge(stg_out[k], 32 * 2 * G)
                for j in range(HPG):
                    if h and j == 1:
                        ln_rstd_part(4)
                    ring_hi_part(R_Q[h], 0, 0, j, ring_hi[:, j % 2, :])
                    if h == 0:
                        if j == 0:
                            scan_prep_w(1, 0, 0)
                            scan_prep(1, 0, 0)
                            scan_prep_ln(1, 0, 0)
                        spread(1, SPREAD * j, SPREAD * (j + 1))
                    hl_part(HL_Q[h], 0, 0, j, q_hi[:, j, :])
                if h == 0:
                    scan_start(1)
                for b in range(2):
                    probs(h, 0, 0, b)
                steps(eng, lambda i, p, nxt: x_step(h, i, p, nxt, h == 0))

            for k in range(2):
                eng.wait_ge(d_free[k], D_FFN // 2)
            for l in range(1 + 2 * KT):
                dst = r_hi[:, :] if l == 0 else a_hi[:, l - 1, :] if l <= KT else b_hi[:, l - 1 - KT, :]
                ring_hi_part(R_FFN, 0, 0, l, dst)
            for h in range(2):
                if h == 0:
                    for k in range(KT):
                        hl_part(HL_LN3[0], 0, 0, k, xt_hi[:, k, :])
                slot, n = use(S_FFN, 0, 0, h)
                eng.wait_ge(s_full[slot], n + 1)
                act(qr[:, :], s_bank[slot][:, :], ACT.Copy).then_inc(s_free[slot], 1)
                eng.wait_ge(gate_f, h + 1)
                for t in range(NB):
                    last = act(ge[:, t, :], sco[:, t, :], ACT.Exp, bias=ntop[:, t:t + 1])
                last.then_inc(ge_ok, 1)
                for k in range(KT):
                    hl_part(HL_ZT[h], 0, 0, k, zt_hi[:, k, :])
                if h == 0:
                    ln_rstd_part(5)
                    for k in range(KT):
                        hl_part(HL_LN3[1], 0, 0, k, xt_hi[:, k, :])

        @block.vector
        def _(eng):
            def lo_part(base, per, i, k, lo, hi):
                slot, n = use(base, per, i, k)
                eng.wait_ge(hl_hi[slot], n + 1)
                nc.vector.tensor_tensor(lo, hl_bank[slot][:, :], hi.bitcast(F32), ALU.subtract).then_inc(
                    hl_free[slot], 1)

            def ln_stats(l, h):
                for t in range(NB):
                    nc.vector.bn_stats(stats[:, t, :], xres[:, NB * h + t, :]).then_inc(ln_mv, 1)
                eng.wait_ge(ln_mv, 2 * NB * l + NB)
                for t in range(NB):
                    last = nc.vector.bn_aggr(mv[:, t, :], stats[:, t, :]).then_inc(ln_mv, 1)
                eng.wait_ge(ln_mv, 2 * NB * l + 2 * NB)
                eng.sem_inc(ln_stat, 1)

            def ln_rows(l, h):
                eng.wait_ge(ln_rstd, 2 * l + 2)
                for t in range(NB):
                    nc.vector.tensor_scalar(xn[:, t, :], xres[:, NB * h + t, :], mv[:, t, 0:1], rstd[:, t:t + 1],
                                            ALU.subtract, ALU.mult).then_inc(ln_xn, 1)

            eng.wait_ge(const_ok, 6)
            nc.vector.tensor_tensor(sel_c[:, :], ident[:, RDT:SSM], ident[:, SSM + RDT:P], ALU.add).then_inc(
                sel_ok, 1)
            eng.wait_ge(sel_ok, 1)
            nc.vector.tensor_copy(sel[:, :, :], sel_c[:, :, None].broadcast_to([P, 2 * NS, P])).then_inc(sel_ok, 1)
            def layer_norm(l, h):
                ln_stats(l, h)
                ln_rows(l, h)

            nc.vector.memset(xpad[:, :, :, 0:TAPS - 1], 0.0).then_inc(zero_ok, 1)
            nc.vector.memset(ssm[:, :, :], 0.0).then_inc(zero_ok, 1)
            for h in range(2):
                eng.wait_ge(x_in[h], 16)
                if h:
                    for k in range(2):
                        eng.wait_ge(hl_full[k], KT // 2)
                layer_norm(h, h)
                for k in range(KT):
                    lo_part(HL_LN1, 0, 0, KT * h + k, (xt_lo, xt1_lo)[h][:, k, :], (xt_hi, xt1_hi)[h][:, k, :])
            nc.vector.memset(da[:, :, :, :], 0.0).then_inc(zero_ok, 1)
            eng.wait_ge(zero_ok, 3)

            eng.wait_ge(w_ok[R_WX % 2], 1)

            def in_step(i, p, nxt):
                c = 2 * i + p
                conv_c = Chain(eng, conv_ch, 6, c)
                for part, w in enumerate((wx_hi, wx_lo)):
                    nc.vector.tensor_copy(wx_step[:, p, part, :],
                                          w[:, bass.ds(SSM * c, SSM)].bitcast(F32)).then_inc(wx_ok, 1)
                eng.wait_ge(cst_in[p], 16 * i + 16)
                for h in range(2):
                    slot, n = use(S_IN + 4 * p, 8, i, h)
                    eng.wait_ge(s_free[slot], n + 1)
                    eng.wait_ge(silu_ok, 2 * c)
                    rows = conv[:, h, :].rearrange("p (b t) -> p b t", b=NB)
                    conv_c.did(nc.vector.tensor_scalar(rows, xpad[:, h, :, 0:SEQ], cst_sb[:, p, CONV0:CONV0 + 1],
                                                       cst_sb[:, p, CONVB:CONVB + 1], ALU.mult, ALU.add))
                    for j in range(1, TAPS):
                        conv_c.wait()
                        ins = nc.vector.scalar_tensor_tensor(
                            out=rows, in0=xpad[:, h, :, j:j + SEQ], scalar=cst_sb[:, p, CONV0 + j:CONV0 + j + 1],
                            in1=rows, op0=ALU.mult, op1=ALU.add)
                        if j < TAPS - 1:
                            conv_c.did(ins)
                        else:
                            ins.then_inc(conv_ok, 1)
                conv_c.end()
                for h in range(2):
                    eng.wait_ge(uhi_ok, 2 * c + h + 1)
                    nc.vector.tensor_tensor(u_lo[:, h, :], u_out[:, p, h, :], u_hi[:, h, :].bitcast(F32),
                                            ALU.subtract).then_inc(ulo_ok, 1)
                for h in range(2):
                    slot, n = use(D_IN + 2 * p, 4, i, h)
                    eng.wait_ge(d_full[slot], n + 1)
                    eng.wait_ge(d_free[slot], n)
                    part = ssm[:, NB * h:NB * (h + 1), :].rearrange("p t n -> p (t n)")
                    nc.vector.tensor_tensor(part, part, d_bank[slot][:, 0:NB * SSM], ALU.add).then_inc(
                        d_free[slot], 1)
            steps(eng, in_step)

            for k in range(2):
                eng.wait_ge(d_free[k], (D_IN + 2 * NC) // 2)
            nc.vector.tensor_tensor(ssm_sq[:, :, :], ssm[:, :, :], ssm[:, :, :], ALU.mult).then_inc(ssm_ch, 1)
            eng.wait_ge(ssm_ch, 1)
            parts = [slice(0, RDT), slice(RDT, RDT + NS), slice(RDT + NS, SSM)]
            for k, cols in enumerate(parts):
                nc.vector.tensor_reduce(ssm_ss[:, k, :], ssm_sq[:, :, cols], AX_X, ALU.add).then_inc(ssm_ch, 1)
            eng.wait_ge(ssm_rs_ok, 3)
            for r in range(2):
                for k, cols in enumerate(parts):
                    n = cols.stop - cols.start
                    nc.vector.tensor_tensor(ssm_n[:, :, r, cols], ssm[:, :, cols],
                                            ssm_rs[:, k, :, None].broadcast_to([P, 2 * NB, n]),
                                            ALU.mult).then_inc(ssm_ch, 1)
            for h in range(2):
                slot, n = use(HL_SSM, 0, 0, h)
                eng.wait_ge(hl_hi[slot], n + 1)
                nc.vector.tensor_tensor(stk[SSM:P, h, :], hl_bank[slot][SSM:P, :], stk_t[SSM:P, :].bitcast(F32),
                                        ALU.subtract).then_inc(hl_free[slot], 1)
            def stage(i, p, k):
                slot, n = use(HL_KV + 4 * p, 8, i, k)
                eng.wait_ge(stg_out[slot], 32 * (n - HL_KV // 2))
                lo_part(HL_KV + 4 * p, 8, i, k, stg_lo[:, slot, :], stg_hi[:, slot, :])

            def kv_step(i, p, nxt):
                scan_chunk(0, i, p, nxt, 3)
                if nxt:
                    scan_prep_a(0, i + p, 1 - p)
                scan_chunk(0, i, p, nxt, 4)
                stage(i, p, 2)
                scan_chunk(0, i, p, nxt, 5)
                if nxt:
                    scan_prep(0, i + p, 1 - p)
                scan_chunk(0, i, p, nxt, 6)
                if nxt:
                    scan_prep_dt(0, i + p, 1 - p)
                stage(i, p, 3)
                scan_chunk(0, i, p, nxt, 7)
                scan_chunk(0, i, p, nxt, 8)
                if nxt:
                    stage(i, p, 4)
                scan_chunk(0, i, p, nxt, 9)
                scan_y(0, i, p)
                scan_y_lo(0, i, p)
                if nxt:
                    stage(i, p, 5)
                scan_add(0, i, p, 0)
                scan_add(0, i, p, 1)
                scan_chunk(0, i, p, nxt, 10)
                scan_add(0, i, p, 2)
                scan_add(0, i, p, 3)

            def scan_prep(h, i, p):
                s = NC * h + 2 * i + p
                eng.wait_ge(ea_ok, s + 1)
                nc.vector.tensor_scalar(B["na"][:, p, :], B["ea"][:, p, :], -1.0, None, ALU.mult).then_inc(na_ok, 1)
                eng.wait_ge(dt_abs, s + 1)
                nc.vector.tensor_scalar(B["rl"][:, :], dt_bank[:, :], cst_sb[:, p, DTB:DTB + 1], 0.0,
                                        ALU.add, ALU.max).then_inc(dt_free, 1)
                eng.wait_ge(dt_exp, 2 * s + 2)
                nc.vector.scalar_tensor_tensor(out=B["sp"][:, :], in0=B["dt"][:, p, :], scalar=1.0, in1=B["sp"][:, :],
                                               op0=ALU.subtract, op1=ALU.subtract).then_inc(dt_err, 1)
                eng.wait_ge(dt_free, s + 1)
                eng.wait_ge(dt_err, s + 1)
                nc.vector.tensor_tensor(B["rl"][:, :], B["rl"][:, :], B["sp"][:, :], ALU.subtract).then_inc(
                    dt_rest, 1)

            def scan_prep_dt(h, i, p):
                s = NC * h + 2 * i + p
                eng.wait_ge(dt_rest, s + 1)
                eng.wait_ge(dt_ln, s + 1)
                nc.vector.tensor_tensor(B["dt"][:, p, :], B["rl"][:, :], B["dt"][:, p, :], ALU.add).then_inc(dt_ok, 1)

            def scan_prep_a(h, i, p):
                n = (NC // 2) * h + i
                eng.wait_ge(scan_in[p], 32 * n + 32)
                nc.vector.tensor_scalar(B["ea"][:, p, :], cst_sb[:, p, 0:NS], A_LOG_MAX, None, ALU.min).then_inc(
                    al_ok, 1)

            def times_c(h, i, p, j):
                s, slot, cs, n = NC * h + 2 * i + p, j % 2, j % 4, NS + CH_N * (j % CHUNKS)
                eng.wait_ge(scan_done[slot], 4 * s + j // 2 + 1)
                nc.vector.tensor_tensor(
                    ch[:, cs, :], ch[:, cs, :],
                    B["bc"][:, n:n + CH_N, :].rearrange("p n t -> p (n t)"),
                    ALU.mult).then_inc(ch_mul[cs], 1)
                if h:
                    eng.wait_ge(ch_mul[cs], 2 * s + j // 4 + 1)
                    nc.vector.tensor_tensor(ch[:, cs, 0:HALF], ch[:, cs, 0:HALF], ch[:, cs, HALF:], ALU.add).then_inc(
                        ch_pair[cs], 1)

            def scan_chunk(h, i, p, nxt, j):
                s, slot, cs = NC * h + 2 * i + p, j % 2, j % 4
                if j < CHUNKS or nxt:
                    eng.wait_ge(da_full[slot], 4 * s + j // 2 + 1)
                    eng.wait_ge(ch_full[cs], 2 * s + j // 4 + 1)
                    nc.vector.tensor_tensor_scan(
                        ch[:, cs, :], da[:, slot, :, :].rearrange("p n t -> p (n t)"), ch[:, cs, :], 0.0,
                        ALU.mult, ALU.add).then_inc(scan_done[slot], 1)
                if j and (j - 1 < CHUNKS or nxt):
                    times_c(h, i, p, j - 1)

            def scan_y(h, i, p):
                s = NC * h + 2 * i + p
                eng.wait_ge(y_full, s + 1)
                eng.wait_ge(sg_in, 16 * s + 16)
                eng.wait_ge(yhi_ok, s)
                eng.wait_ge(ylo_ok, s)
                nc.vector.scalar_tensor_tensor(out=B["y"][:, :], in0=B["u"][:, p, :],
                                               scalar=cst_sb[:, p, DSKIP:DSKIP + 1], in1=y_bank[:, :],
                                               op0=ALU.mult, op1=ALU.add).then_inc(y_free, 1)
                eng.wait_ge(y_free, s + 1)
                nc.vector.tensor_tensor(B["y"][:, :], B["y"][:, :], B["sg"][:, :], ALU.mult).then_inc(y_ok, 1)

            def scan_y_lo(h, i, p):
                s = NC * h + 2 * i + p
                eng.wait_ge(yhi_ok, s + 1)
                nc.vector.tensor_tensor(B["y_lo"][:, :], B["y"][:, :], B["y_hi"][:, :].bitcast(F32),
                                        ALU.subtract).then_inc(ylo_ok, 1)

            def scan_add(h, i, p, t):
                add_to_x(D_SCAN[h] + D_SCAN_PER[h] * p, 2 * D_SCAN_PER[h], i, t, NB * h + t)

            def add_to_x(base, per, i, k, t):
                slot, n = use(base, per, i, k)
                eng.wait_ge(d_full[slot], n + 1)
                eng.wait_ge(d_free[slot], n - 1)
                nc.vector.tensor_tensor(xres[:, t, :], xres[:, t, :], d_bank[slot][:, :], ALU.add).then_inc(
                    d_free[slot], 1)

            def spread(h, first, last):
                for k in range(first, last):
                    slot, n = use(D_BC[h], 0, 0, k)
                    eng.wait_ge(d_full[slot], n + 1)
                    nc.vector.tensor_copy(B["bc"][:, 2 * k + 1, :], d_bank[slot][:, :]).then_inc(d_free[slot], 1)

            def scan_start(h):
                for k in range(2):
                    eng.wait_ge(s_free[k], (S_BC[h] + NS) // 2)
                    eng.wait_ge(d_free[k], (D_BC[h] + NS) // 2)
                for j in range(3):
                    scan_chunk(h, 0, 0, True, j)

            def row_max(h, i, p, b):
                slot, n = use(S_X[h] + NB * p, 2 * NB, i, b)
                eng.wait_ge(s_full[slot], n + 1)
                nc.vector.tensor_reduce(mx[:, b % 2, :], s_bank[slot][:, :].rearrange("p (h k) -> p h k", h=HPG),
                                        AX_X, ALU.max).then_inc(mx_ch, 1)
                eng.wait_ge(mx_ch, NB * (G * h + 2 * i + p) + b + 1)
                nc.vector.tensor_scalar(nmx[:, b % 2, :], mx[:, b % 2, :], -DK ** -0.5, None,
                                        ALU.mult).then_inc(mx_ok, 1)

            def recip(h, i, p, b):
                slot, n = use(S_X[h] + NB * p, 2 * NB, i, b)
                eng.wait_ge(sum_ok, NB * (G * h + 2 * i + p) + b + 1)
                nc.vector.reciprocal(rcp[:, b % 2, :], psum_row[:, b % 2, :]).then_inc(rcp_ok, 1)
                eng.sem_inc(s_free[slot], 1)

            def x_step(h, i, p, nxt, scan=False):
                def chunk(j):
                    if scan:
                        scan_chunk(1, i, p, nxt, j)

                def lo(k, lo_, hi_):
                    lo_part(HL_X[h] + XSTEP * p, 2 * XSTEP, i, k, lo_, hi_)

                def turned(b):
                    lo(PT_AT[nxt][b], pt_lo[:, :], pt_hi[:, :])

                def attended(b):
                    lo(AT_AT[nxt][b], at_lo[:, b % 2, :], at_hi[:, b % 2, :])

                def next_q(j):
                    if nxt:
                        lo(Q_AT[j], q_lo[:, j, :], q_hi[:, j, :])

                def x_add(b):
                    add_to_x(D_X[h] + D_X_PER[h] * p, 2 * D_X_PER[h], i, b, NB * h + b)

                turned(0)
                row_max(h, i, p, 2)
                if scan and nxt:
                    scan_prep_a(1, i + p, 1 - p)
                attended(0)
                recip(h, i, p, 2)
                turned(1)
                row_max(h, i, p, 3)
                chunk(3)
                attended(1)
                chunk(4)
                turned(2)
                recip(h, i, p, 3)
                next_q(0)
                chunk(5)
                if scan and nxt:
                    scan_prep(1, i + p, 1 - p)
                x_add(0)
                next_q(1)
                chunk(6)
                if scan and nxt:
                    scan_prep_dt(1, i + p, 1 - p)
                attended(2)
                x_add(1)
                chunk(7)
                turned(3)
                next_q(2)
                chunk(8)
                attended(3)
                next_q(3)
                chunk(9)
                if scan:
                    scan_y(1, i, p)
                x_add(2)
                if nxt:
                    row_max(h, i, p, NB)
                if scan:
                    scan_y_lo(1, i, p)
                if nxt:
                    row_max(h, i, p, NB + 1)
                if nxt:
                    recip(h, i, p, NB)
                x_add(3)
                if nxt:
                    chunk(10)
                    recip(h, i, p, NB + 1)
                if scan:
                    for t in range(NB):
                        scan_add(1, i, p, t)

            scan_prep_a(0, 0, 0)
            scan_prep(0, 0, 0)
            scan_prep_dt(0, 0, 0)
            spread(0, 0, NS)
            scan_start(0)
            for k in range(2):
                stage(0, 0, k)
            steps(eng, kv_step)
            for k in range(2):
                eng.wait_ge(d_free[k], D_BC[1] // 2)
                for slot in range(4):
                    eng.wait_ge(ch_free[slot], 2 * NC)
            for h in range(2):
                if h:
                    for k in range(2):
                        eng.wait_ge(d_free[k], D_X[1] // 2)
                        eng.wait_ge(ch_free[k], 2 * 2 * NC)
                        eng.wait_ge(hl_full[k], HL_LN2[1] // 2)
                layer_norm(2 + h, h)
                for k in range(KT):
                    lo_part(HL_LN2[h], 0, 0, k, xt_lo[:, k, :], xt_hi[:, k, :])
                if h == 0:
                    for k in range(2):
                        eng.wait_ge(stg_out[k], 32 * 2 * G)
                if h:
                    ln_stats(4, 0)
                for j in range(HPG):
                    if h and j == 1:
                        ln_rows(4, 0)
                    if h == 0:
                        if j == 0:
                            scan_prep_a(1, 0, 0)
                            scan_prep(1, 0, 0)
                            scan_prep_dt(1, 0, 0)
                        spread(1, SPREAD * j, SPREAD * (j + 1))
                    lo_part(HL_Q[h], 0, 0, j, q_lo[:, j, :], q_hi[:, j, :])
                if h == 0:
                    scan_start(1)
                for b in range(2):
                    row_max(h, 0, 0, b)
                for b in range(2):
                    recip(h, 0, 0, b)
                steps(eng, lambda i, p, nxt: x_step(h, i, p, nxt, h == 0))

            for k in range(2):
                eng.wait_ge(d_free[k], D_FFN // 2)
            def rows_lo(h):
                for k in range(KT):
                    lo_part(HL_LN3[h], 0, 0, k, xt_lo[:, k, :], xt_hi[:, k, :])

            for h in range(2):
                f = Chain(eng, ffn_ch, 6 * NB + 3, h)
                if h == 0:
                    rows_lo(0)
                slot, n = use(D_FFN, 0, 0, (2 * NB + 1) * h)
                eng.wait_ge(d_full[slot], n + 1)
                if h:
                    eng.wait_ge(ge_ok, h)
                nc.vector.tensor_copy(sco[:, :, :].rearrange("p t e -> p (t e)"),
                                      d_bank[slot][:, 0:NB * EXPERTS]).then_inc(d_free[slot], 1)
                eng.wait_ge(d_free[slot], n + 1)
                for t in range(NB):
                    f.did(nc.vector.max(out=top[:, t, 0, :], in_=sco[:, t, :]))
                f.wait()
                nc.vector.tensor_scalar(ntop[:, :], top[:, :, 0, 0], -1.0, None, ALU.mult).then_inc(gate_f, 1)
                for t in range(NB):
                    f.did(nc.vector.match_replace(out=sco1[:, t, :], in_to_replace=top[:, t, 0, :],
                                                  in_values=sco[:, t, :], imm_value=NEG))
                f.wait()
                for t in range(NB):
                    f.did(nc.vector.max(out=top[:, t, 1, :], in_=sco1[:, t, :]))
                f.wait()
                for t in range(NB):
                    f.did(nc.vector.match_replace(out=sco2[:, t, :], in_to_replace=top[:, t, 1, :],
                                                  in_values=sco1[:, t, :], imm_value=NEG))
                f.wait()
                f.did(nc.vector.tensor_scalar(picked[:, :, :], sco2[:, :, :], NEG, None, ALU.is_equal))
                f.wait()
                eng.wait_ge(ge_ok, h + 1)
                f.did(nc.vector.tensor_tensor(picked[:, :, :], picked[:, :, :], ge[:, :, :], ALU.mult))
                f.wait()
                f.did(nc.vector.tensor_reduce(gsum[:, :], picked[:, :, :], AX_X, ALU.add))
                f.wait()
                for t in range(NB):
                    f.did(nc.vector.reciprocal(grcp[:, t:t + 1], gsum[:, t:t + 1]))
                f.wait()
                for t in range(NB):
                    f.did(nc.vector.tensor_scalar(picked[:, t, :], picked[:, t, :], grcp[:, t:t + 1], None, ALU.mult))
                f.wait()
                f.end()
                if h:
                    for k in range(2):
                        eng.wait_ge(hl_full[k], HL_LN3[h] // 2)
                for t in range(NB):
                    slot, n = use(D_FFN, 0, 0, (2 * NB + 1) * h + 1 + t)
                    eng.wait_ge(d_full[slot], n + 1)
                    nc.vector.tensor_tensor(zg[:, t, :].rearrange("p (e r) -> p e r", r=RANK),
                                            d_bank[slot][:, :].rearrange("p (e r) -> p e r", r=RANK),
                                            picked[:, t, :, None].broadcast_to([P, EXPERTS, RANK]),
                                            ALU.mult).then_inc(d_free[slot], 1)
                if h == 0:
                    ln_stats(5, 1)
                for k in range(KT):
                    lo_part(HL_ZT[h], 0, 0, k, zt_lo[:, k, :], zt_hi[:, k, :])
                if h == 0:
                    ln_rows(5, 1)
                    rows_lo(1)
                for t in range(NB):
                    slot, n = use(D_FFN, 0, 0, (2 * NB + 1) * h + 1 + NB + t)
                    eng.wait_ge(d_full[slot], n + 1)
                    nc.vector.scalar_tensor_tensor(out=res[:, NB * h + t, :], in0=d_bank[slot][:, :], scalar=2.0,
                                                   in1=xres[:, NB * h + t, :], op0=ALU.mult,
                                                   op1=ALU.add).then_inc(out_ok, 1)
                    eng.wait_ge(out_ok, NB * h + t + 1)
                    eng.sem_inc(d_free[slot], 1)

        @block.tensor
        def _(eng):
            mm = nc.tensor.matmul

            def begin(kind_free, base, per, i, k):
                slot, n = use(base, per, i, k)
                eng.wait_ge(kind_free[slot], n)
                return slot

            def three(dst, w_hi, w_lo, m_hi, m_lo, first, last):
                mm(dst, w_hi, m_hi, start=first, stop=False)
                mm(dst, w_lo, m_hi, start=False, stop=False)
                return mm(dst, w_hi, m_lo, start=False, stop=last)

            def over_k(dst, w, m):
                for k in range(KT):
                    ins = three(dst, w[0](k), w[1](k), m[0](k), m[1](k), k == 0, k == KT - 1)
                return ins

            def transposes(slot, src):
                for t in range(NB):
                    ins = nc.tensor.transpose(hl_bank[slot][:, P * t:P * (t + 1)], src(t), ident[:, :])
                ins.then_inc(hl_full[slot], 1)

            def layer_norm(l, base, k0):
                eng.wait_ge(ln_xn, NB * l + NB)
                for k in range(KT):
                    slot = begin(hl_free, base, 0, 0, k0 + k)
                    transposes(slot, lambda t: xn[:, t, P * k:P * (k + 1)])

            def ring(slot):
                return (lambda k: ring_hi[:, slot, P * k:P * (k + 1)]), (lambda k: ring_lo[:, slot, P * k:P * (k + 1)])

            def ring_ready(base, per, i, k):
                slot, n = use(base, per, i, k)
                eng.wait_ge(w_ok[slot], n + 1)

            eng.wait_ge(const_ok, 6)
            for h in range(2):
                layer_norm(h, HL_LN1, KT * h)
            for k in range(2):
                eng.wait_ge(hl_free[k], (HL_LN1 + 2 * KT) // 2)
            xts = [((lambda k: xt_hi[:, k, :]), (lambda k: xt_lo[:, k, :])),
                   ((lambda k: xt1_hi[:, k, :]), (lambda k: xt1_lo[:, k, :]))]

            def in_part(i, p, k):
                h, part = k % 2, (k // 2) % 2
                if h == 0:
                    ring_ready(R_IN + 2 * p, 4, i, k // 2)
                slot = begin(s_free, S_IN + 4 * p, 8, i, k)
                over_k(s_bank[slot][:, :], ring(part), xts[h]).then_inc(s_full[slot], 1)

            def in_step(i, p, nxt):
                c = 2 * i + p
                for k in range(2, 6 if nxt else 4):
                    in_part(i, p, k)
                eng.wait_ge(wx_ok, 2 * c + 2)
                for h in range(2):
                    slot = begin(d_free, D_IN + 2 * p, 4, i, h)
                    eng.wait_ge(ulo_ok, 2 * c + h + 1)
                    for t in range(NB):
                        rows = slice(P * t, P * (t + 1))
                        ins = three(d_bank[slot][:, SSM * t:SSM * (t + 1)], u_hi[:, h, rows], u_lo[:, h, rows],
                                    wx_step[:, p, 0, :], wx_step[:, p, 1, :], True, True)
                    ins.then_inc(d_full[slot], 1)

            ring_ready(R_IN0, 0, 0, 0)
            for k in range(2):
                in_part(0, 0, k)
            steps(eng, in_step)

            eng.wait_ge(ssm_ch, 4 + 6)
            for h in range(2):
                slot = begin(hl_free, HL_SSM, 0, 0, h)
                transposes(slot, lambda t: ssm_n[:, NB * h + t, :, :].rearrange("p a n -> p (a n)"))

            def kv_job(i, p, k):
                part, h = (k // 2) % 2, k % 2
                if h == 0:
                    ring_ready(R_KV + 2 * p, 4, i, k // 2)
                slot = begin(hl_free, HL_KV + 4 * p, 8, i, k)
                if part == 0:
                    ins = over_k(hl_bank[slot][:, :], ring(0),
                                 ((lambda q: ctx_hi[:, q, HALF * h:HALF * (h + 1)]),
                                  (lambda q: ctx_lo[:, q, HALF * h:HALF * (h + 1)])))
                else:
                    for t in range(NB):
                        rows = slice(HALF * h + P * t, HALF * h + P * (t + 1))
                        ins = over_k(hl_bank[slot][:, DK * t:DK * (t + 1)],
                                     ((lambda q: ctx_hi[:, q, rows]), (lambda q: ctx_lo[:, q, rows])), ring(1))
                ins.then_inc(hl_full[slot], 1)

            def kv_step(i, p, nxt):
                scan_sum(0, i, p, 0)
                scan_sum(0, i, p, 1)
                kv_job(i, p, 2)
                if nxt:
                    scan_prep(0, i + p, 1 - p)
                scan_sum(0, i, p, 2)
                scan_sum(0, i, p, 3)
                kv_job(i, p, 3)
                scan_sum(0, i, p, 4)
                scan_sum(0, i, p, 5)
                if nxt:
                    kv_job(i, p, 4)
                scan_sum(0, i, p, 6)
                scan_sum(0, i, p, 7)
                if nxt:
                    kv_job(i, p, 5)
                scan_out(0, i, p)

            def scan_prep(h, i, p):
                s = NC * h + 2 * i + p
                eng.wait_ge(wdt_ok, s + 1)
                eng.wait_ge(dt_free, s)
                mm(dt_bank[:, :], B["wdt_hi"][:, :], stk[:, h, :], start=True, stop=False)
                mm(dt_bank[:, :], B["wdt_lo"][:, :], stk[:, h, :], start=False, stop=True).then_inc(dt_full, 1)

            def scan_sum(h, i, p, j):
                s, cs = NC * h + 2 * i + p, j % 4
                if j == 0:
                    eng.wait_ge(y_free, s)
                if h:
                    eng.wait_ge(ch_pair[cs], 2 * (s - NC) + j // 4 + 1)
                else:
                    eng.wait_ge(ch_mul[cs], 2 * s + j // 4 + 1)
                parts = 1 if h else CH_N
                for m in range(parts):
                    ins = mm(y_bank[:, :], ident[:, :], ch[:, cs, HALF * m:HALF * (m + 1)],
                             start=(j == 0 and m == 0), stop=(j == CHUNKS - 1 and m == parts - 1))
                ins.then_inc(ch_free[cs], 1)
                if j == CHUNKS - 1:
                    eng.wait_ge(ch_free[cs], 2 * s + 2)
                    eng.sem_inc(y_full, 1)

            def scan_out(h, i, p):
                s, per = NC * h + 2 * i + p, D_SCAN_PER[h]
                eng.wait_ge(wo_ok, s + 1)
                eng.wait_ge(ylo_ok, s + 1)
                for t in range(NB):
                    slot = begin(d_free, D_SCAN[h] + per * p, 2 * per, i, t)
                    rows = slice(P * t, P * (t + 1))
                    three(d_bank[slot][:, :], B["y_hi"][:, rows], B["y_lo"][:, rows], B["wo_hi"][:, :],
                          B["wo_lo"][:, :], True, True).then_inc(d_full[slot], 1)

            def spread(h, first, last):
                for k in range(first, last):
                    slot = begin(s_free, S_BC[h], 0, 0, k)
                    mm(s_bank[slot][:, :], sel[:, 2 * k, :], stk[:, h, :], start=True, stop=True).then_inc(
                        s_full[slot], 1)
                    slot = begin(d_free, D_BC[h], 0, 0, k)
                    mm(d_bank[slot][:, :], sel[:, 2 * k + 1, :], stk[:, h, :], start=True, stop=True).then_inc(
                        d_full[slot], 1)

            def project_q(base, per, i, k, rbase, rper, rk, j):
                ring_ready(rbase, rper, i, rk)
                slot = begin(hl_free, base, per, i, k)
                over_k(hl_bank[slot][:, :], ring(j % 2), xts[0]).then_inc(hl_full[slot], 1)

            def scores(h, i, p, b):
                slot = begin(s_free, S_X[h] + NB * p, 2 * NB, i, b)
                rows = slice(P * (b % NB), P * (b % NB + 1))
                mm(s_bank[slot][:, :].rearrange("p (h k) -> p h k", h=HPG), ident_r[:, :],
                   mask_r[:, None, :].broadcast_to([P, HPG, P]), start=True, stop=False)
                for j in range(HPG):
                    ins = three(s_bank[slot][:, P * j:P * (j + 1)], q_hi[:, j, rows], q_lo[:, j, rows],
                                kv[:, 0, 0, rows], kv[:, 0, 1, rows], False, j == HPG - 1)
                ins.then_inc(s_full[slot], 1)

            def x_step(h, i, p, nxt, scan=False):
                s = G * h + 2 * i + p
                hb, hper = HL_X[h] + XSTEP * p, 2 * XSTEP

                def chunk(j):
                    if scan:
                        scan_sum(1, i, p, j)

                def turn(b):
                    eng.wait_ge(pn_ok, NB * s + b + 1)
                    slot = begin(hl_free, hb, hper, i, PT_AT[nxt][b])
                    transposes(slot, lambda j: pr[:, b % 2, j, :])

                def attend(b):
                    sl, n = use(hb, hper, i, PT_AT[nxt][b])
                    eng.wait_ge(hl_free[sl], n + 1)
                    if b == 0:
                        eng.wait_ge(v_in, 16 * s + 16)
                    slot = begin(hl_free, hb, hper, i, AT_AT[nxt][b])
                    rows = slice(P * b, P * (b + 1))
                    three(hl_bank[slot][:, :], kv[:, 1, 0, rows], kv[:, 1, 1, rows], pt_hi[:, :], pt_lo[:, :],
                          True, True).then_inc(hl_full[slot], 1)

                def project_out(b):
                    sl, n = use(hb, hper, i, AT_AT[nxt][b])
                    eng.wait_ge(hl_free[sl], n + 1)
                    if b == 0:
                        eng.wait_ge(wd_ok, HPG * s + HPG)
                    slot = begin(d_free, D_X[h] + D_X_PER[h] * p, 2 * D_X_PER[h], i, b)
                    for j in range(HPG):
                        cols = slice(P * j, P * (j + 1))
                        ins = three(d_bank[slot][:, :], at_hi[:, b % 2, cols], at_lo[:, b % 2, cols],
                                    wd_hi[:, j, :], wd_lo[:, j, :], j == 0, j == HPG - 1)
                    ins.then_inc(d_full[slot], 1)

                def next_q(j):
                    if nxt:
                        project_q(hb, hper, i, Q_AT[j], R_X[h] + HPG * p, 2 * HPG, j, j)

                turn(0)
                scores(h, i, p, 2)
                chunk(0)
                attend(0)
                turn(1)
                scores(h, i, p, 3)
                chunk(1)
                attend(1)
                turn(2)
                if scan and nxt:
                    scan_prep(1, i + p, 1 - p)
                chunk(2)
                next_q(0)
                chunk(3)
                project_out(0)
                next_q(1)
                chunk(4)
                attend(2)
                project_out(1)
                chunk(5)
                turn(3)
                next_q(2)
                chunk(6)
                attend(3)
                next_q(3)
                chunk(7)
                project_out(2)
                if nxt:
                    eng.wait_ge(k_in, 16 * s + 32)
                    for k in range(2):
                        eng.wait_ge(hl_free[k], hb // 2 + XSTEP * i + XSTEP // 2)
                    scores(h, i, p, NB)
                    scores(h, i, p, NB + 1)
                project_out(3)
                if scan:
                    scan_out(1, i, p)

            eng.wait_ge(sel_ok, 2)
            scan_prep(0, 0, 0)
            spread(0, 0, NS)
            kv_job(0, 0, 0)
            kv_job(0, 0, 1)
            steps(eng, kv_step)
            for h in range(2):
                layer_norm(2 + h, HL_LN2[h], 0)
                for k in range(2):
                    eng.wait_ge(hl_free[k], HL_Q[h] // 2)
                if h == 0:
                    scan_prep(1, 0, 0)
                for j in range(HPG):
                    if h == 0:
                        spread(1, SPREAD * j, SPREAD * (j + 1))
                    project_q(HL_Q[h], 0, 0, j, R_Q[h], 0, j, j)
                eng.wait_ge(k_in, 16 * G * h + 16)
                for k in range(2):
                    eng.wait_ge(hl_free[k], HL_X[h] // 2)
                scores(h, 0, 0, 0)
                scores(h, 0, 0, 1)
                steps(eng, lambda i, p, nxt: x_step(h, i, p, nxt, h == 0))

            for h in range(2):
                if h == 0:
                    layer_norm(4, HL_LN3[0], 0)
                for k in range(2):
                    eng.wait_ge(hl_free[k], HL_ZT[h] // 2)
                ring_ready(R_FFN, 0, 0, 0)
                slot = begin(s_free, S_FFN, 0, 0, h)
                over_k(s_bank[slot][:, :], ((lambda k: r_hi[:, P * k:P * (k + 1)]),
                                            (lambda k: r_lo[:, P * k:P * (k + 1)])), xts[0]).then_inc(s_full[slot], 1)
                eng.wait_ge(keys_in, 16)
                eng.wait_ge(s_free[slot], use(S_FFN, 0, 0, h)[1] + 1)
                slot = begin(d_free, D_FFN, 0, 0, (2 * NB + 1) * h)
                for t in range(NB):
                    ins = mm(d_bank[slot][:, EXPERTS * t:EXPERTS * (t + 1)], qr[:, P * t:P * (t + 1)], keys_sb[:, :],
                             start=True, stop=True)
                ins.then_inc(d_full[slot], 1)
                for k in range(KT):
                    ring_ready(R_FFN, 0, 0, 1 + k)
                for t in range(NB):
                    slot = begin(d_free, D_FFN, 0, 0, (2 * NB + 1) * h + 1 + t)
                    rows = slice(P * t, P * (t + 1))
                    over_k(d_bank[slot][:, :], ((lambda k: xt_hi[:, k, rows]), (lambda k: xt_lo[:, k, rows])),
                           ((lambda k: a_hi[:, k, :]), (lambda k: a_lo[:, k, :]))).then_inc(d_full[slot], 1)
                for k in range(2):
                    eng.wait_ge(d_free[k], (D_FFN + (2 * NB + 1) * h + 1 + NB + 1 - k) // 2)
                for k in range(KT):
                    slot = begin(hl_free, HL_ZT[h], 0, 0, k)
                    transposes(slot, lambda t: zg[:, t, P * k:P * (k + 1)])
                if h == 0:
                    layer_norm(5, HL_LN3[1], 0)
                for k in range(2):
                    eng.wait_ge(hl_free[k], (HL_ZT[h] + KT) // 2)
                for k in range(KT):
                    ring_ready(R_FFN, 0, 0, 1 + KT + k)
                for t in range(NB):
                    slot = begin(d_free, D_FFN, 0, 0, (2 * NB + 1) * h + 1 + NB + t)
                    rows = slice(P * t, P * (t + 1))
                    over_k(d_bank[slot][:, :], ((lambda k: zt_hi[:, k, rows]), (lambda k: zt_lo[:, k, rows])),
                           ((lambda k: b_hi[:, k, :]), (lambda k: b_lo[:, k, :]))).then_inc(d_full[slot], 1)


PT_AT = {True: [0, 2, 4, 8], False: [0, 2, 4, 6]}
AT_AT = {True: [1, 3, 7, 10], False: [1, 3, 5, 7]}
Q_AT = [5, 6, 9, 11]


def kernel(**inputs):
    import concourse.bacc as bacc
    from concourse.bass_utils import run_bass_kernel_spmd

    a = {k: np.asarray(v) for k, v in inputs.items()}

    def tiles(w):
        k = w.shape[0] // P
        return w.reshape(k, P, w.shape[1]).transpose(1, 0, 2).reshape(P, -1)

    def rows(x):
        return x.reshape(2, NB, P, DM).transpose(0, 2, 1, 3)

    w_in_t = a["L0_attn_W_in"].T
    w_in = np.stack([np.stack([tiles(w_in_t[:, DIN * part + P * c:DIN * part + P * (c + 1)]) for part in range(2)])
                     for c in range(NC)])
    cst = np.concatenate([a["L0_attn_A_log"], a["L0_attn_conv_w"], a["L0_attn_conv_b"][:, None],
                          a["L0_attn_b_dt"][:, None], a["L0_attn_D"][:, None]], axis=1).reshape(NC, P, CST)
    w_dt = np.zeros((NC, P, P), np.float32)
    dt_t = a["L0_attn_W_dt"].T.reshape(RDT, NC, P).transpose(1, 0, 2)
    w_dt[:, 0:RDT] = dt_t
    w_dt[:, SSM:SSM + RDT] = dt_t
    ctx_t = a["ctx_4096"].reshape(TOK, DM).T.reshape(KT, P, 2, HALF).transpose(0, 2, 1, 3).reshape(2 * KT, P, HALF)
    wk_t, wv_t, wq_t = a["L0_xattn_Wk"].T, a["L0_xattn_Wv"].T, a["L0_xattn_Wq"].T
    w_kv = np.stack([np.stack([tiles(w[:, DK * g:DK * (g + 1)]) for w in (wk_t, wv_t)]) for g in range(G)])
    w_q = np.stack([np.stack([tiles(wq_t[:, DK * (HPG * g + j):DK * (HPG * g + j + 1)]) for j in range(HPG)])
                    for g in range(G)])
    w_r = np.zeros((DM, P), np.float32)
    w_r[:, 0:RDIM] = a["L0_ffn_Wq_w"].T
    keys = np.zeros((P, EXPERTS), np.float32)
    keys[0:RDIM] = a["L0_ffn_keys"].T
    arrays = {
        "x": rows(a["x"].reshape(TOK, DM)),
        "w_in": w_in,
        "cst": cst,
        "w_x": tiles(a["L0_attn_W_x"].T),
        "w_dt": w_dt,
        "w_out": a["L0_attn_W_out"].T.reshape(NC, P, DM),
        "ctx_t": ctx_t,
        "w_kv": w_kv,
        "w_q": w_q,
        "w_d": a["L0_xattn_Wd"].T.reshape(G, HPG, P, DM).transpose(0, 2, 1, 3),
        "w_a": a["L0_ffn_A_w"].T.reshape(KT, P, DM),
        "w_b": a["L0_ffn_B_w"].T.reshape(KT, P, DM),
        "w_r": tiles(w_r),
        "keys": keys,
    }
    nc = bacc.Bacc("TRN2", target_bir_lowering=False, num_devices=1, dynamic_dma_scratch_size=1024)
    args, given = [], {}
    for name, v in arrays.items():
        given[f"in_{name}"] = np.ascontiguousarray(v)
        args.append(nc.dram_tensor(f"in_{name}", v.shape, F32, kind="ExternalInput").ap())
    args.append(nc.dram_tensor("out_rows", (2, P, NB, DM), F32, kind="ExternalOutput").ap())
    bass_decoder(nc, *args)
    r = run_bass_kernel_spmd(nc, [given], core_ids=[0])
    got = r.results[0]["out_rows"]
    return np.ascontiguousarray(got.transpose(0, 2, 1, 3)).reshape(BATCH, SEQ, DM)
```
